# Optimizing a Trainium2 kernel written in Bass

```python
import numpy as np
import jax
import jax.numpy as jnp

def _softmax(x, axis=-1):
    return jax.nn.softmax(x, axis=axis)

def _gelu(x):
    return jax.nn.gelu(x, approximate=True)

def _silu(x):
    return jax.nn.silu(x)

def _sigmoid(x):
    return jax.nn.sigmoid(x)

def _layernorm(x, axis=-1, eps=1e-05):
    m = jnp.mean(x, axis=axis, keepdims=True)
    v = jnp.var(x, axis=axis, keepdims=True)
    return (x - m) / jnp.sqrt(v + eps)

def _scatter_add(tgt, idx, src, axis=0):
    return tgt.at[idx].add(src)

def _segment_sum(src, seg, n):
    return jax.ops.segment_sum(src, seg, n)
kernel_name = 'mk_seq_preln_d1_jaxref_r8_76c04f'

def setup_inputs(seed: int=0):
    np.random.seed(seed)
    _w = jnp.asarray

    def _L0_attn_setup():
        import jax, jax.numpy as jnp
        import numpy as np
        D_MODEL = 128
        H = 16
        DH = D_MODEL // H
        WIN = 7
        PAD = WIN // 2
        B, L = (2, 512)
        key = jax.random.key(seed)
        ks = jax.random.split(key, 12)
        s = lambda k, shape: jax.random.normal(k, shape, dtype=jnp.float32) * 0.02
        return {'x': jax.random.normal(ks[0], (B, L, D_MODEL), dtype=jnp.float32), 'wq': s(ks[1], (D_MODEL, D_MODEL)), 'wk': s(ks[2], (D_MODEL, D_MODEL)), 'wv': s(ks[3], (D_MODEL, D_MODEL)), 'wo': s(ks[4], (D_MODEL, D_MODEL)), 'bo': s(ks[5], (D_MODEL,)), 'cw1': s(ks[6], (H, 32, 1)), 'cb1': s(ks[7], (H, 32)), 'cw2': s(ks[8], (H, 32, 32)), 'cb2': s(ks[9], (H, 32)), 'cw3': s(ks[10], (H, 1, 32)), 'cb3': s(ks[11], (H, 1))}
    _L0_attn_in = _L0_attn_setup()

    def _L0_ffn_setup():
        import jax, jax.numpy as jnp
        import numpy as np
        HIDDEN = 128
        FFN = 512
        NUM_EXPERTS = 8
        TOP_K = 2
        BATCH, SEQ = (2, 256)
        key = jax.random.key(seed)
        ks = jax.random.split(key, 6)
        s_h = 1.0 / np.sqrt(HIDDEN)
        s_f = 1.0 / np.sqrt(FFN)
        return {'hidden_states': jax.random.normal(ks[0], (BATCH, SEQ, HIDDEN), jnp.float32), 'gate_w': jax.random.uniform(ks[1], (HIDDEN, NUM_EXPERTS), jnp.float32, -s_h, s_h), 'gate_b': jax.random.uniform(ks[2], (NUM_EXPERTS,), jnp.float32, -s_h, s_h), 'w1': jax.random.uniform(ks[3], (NUM_EXPERTS, HIDDEN, FFN), jnp.float32, -s_h, s_h), 'w3': jax.random.uniform(ks[4], (NUM_EXPERTS, HIDDEN, FFN), jnp.float32, -s_h, s_h), 'w2': jax.random.uniform(ks[5], (NUM_EXPERTS, FFN, HIDDEN), jnp.float32, -s_f, s_f)}
    _L0_ffn_in = _L0_ffn_setup()
    _d = {'L0_attn_x': _L0_attn_in['x'], 'L0_attn_wq': _L0_attn_in['wq'], 'L0_attn_wk': _L0_attn_in['wk'], 'L0_attn_wv': _L0_attn_in['wv'], 'L0_attn_wo': _L0_attn_in['wo'], 'L0_attn_bo': _L0_attn_in['bo'], 'L0_attn_cw1': _L0_attn_in['cw1'], 'L0_attn_cb1': _L0_attn_in['cb1'], 'L0_attn_cw2': _L0_attn_in['cw2'], 'L0_attn_cb2': _L0_attn_in['cb2'], 'L0_attn_cw3': _L0_attn_in['cw3'], 'L0_attn_cb3': _L0_attn_in['cb3'], 'L0_ffn_gate_w': _L0_ffn_in['gate_w'], 'L0_ffn_gate_b': _L0_ffn_in['gate_b'], 'L0_ffn_w1': _L0_ffn_in['w1'], 'L0_ffn_w3': _L0_ffn_in['w3'], 'L0_ffn_w2': _L0_ffn_in['w2']}
    _x0 = _d['L0_attn_x']
    _d['L0_attn_x'] = jax.random.normal(jax.random.fold_in(jax.random.key(seed), 1), (4, 1024, 128), dtype=_x0.dtype)
    del _x0
    return _d

def reference(L0_attn_x, L0_attn_wq, L0_attn_wk, L0_attn_wv, L0_attn_wo, L0_attn_bo, L0_attn_cw1, L0_attn_cb1, L0_attn_cw2, L0_attn_cb2, L0_attn_cw3, L0_attn_cb3, L0_ffn_gate_w, L0_ffn_gate_b, L0_ffn_w1, L0_ffn_w3, L0_ffn_w2):

    def _L0_attn_ref(x, wq, wk, wv, wo, bo, cw1, cb1, cw2, cb2, cw3, cb3):
        import jax, jax.numpy as jnp
        import numpy as np
        D_MODEL = 128
        H = 16
        DH = D_MODEL // H
        WIN = 7
        PAD = WIN // 2
        B, L = (2, 512)
        b, l, d = x.shape

        def heads(w):
            return (x @ w.T).reshape(b, l, H, DH).transpose(0, 2, 1, 3)
        Q, K, V = (heads(wq), heads(wk), heads(wv))
        Kp = jnp.pad(K, ((0, 0), (0, 0), (PAD, PAD), (0, 0)))
        Vp = jnp.pad(V, ((0, 0), (0, 0), (PAD, PAD), (0, 0)))
        idx = jnp.arange(l)[:, None] + jnp.arange(WIN)[None, :]
        Kw = Kp[:, :, idx]
        Vw = Vp[:, :, idx]
        scores = jnp.einsum('bhld,bhlwd->bhlw', Q, Kw) / np.float32(np.sqrt(DH))
        attn = jax.nn.softmax(scores, axis=-1)
        pos = jnp.linspace(0.0, 1.0, WIN, dtype=jnp.float32)[:, None]
        gelu = lambda z: jax.nn.gelu(z, approximate=False)
        h = gelu(jnp.einsum('wi,hji->hwj', pos, cw1) + cb1[:, None, :])
        h = gelu(jnp.einsum('hwi,hji->hwj', h, cw2) + cb2[:, None, :])
        cwt = (jnp.einsum('hwi,hji->hwj', h, cw3) + cb3[:, None, :])[..., 0]
        conn = jax.nn.softmax(cwt, axis=-1)[None, :, None, :]
        fw = attn * conn
        fw = fw / (fw.sum(axis=-1, keepdims=True) + 1e-09)
        out = jnp.einsum('bhlw,bhlwd->bhld', fw, Vw)
        out = out.transpose(0, 2, 1, 3).reshape(b, l, d)
        return out @ wo.T + bo

    def _L0_ffn_ref(hidden_states, gate_w, gate_b, w1, w3, w2):
        import jax, jax.numpy as jnp
        import numpy as np
        HIDDEN = 128
        FFN = 512
        NUM_EXPERTS = 8
        TOP_K = 2
        BATCH, SEQ = (2, 256)
        B, S, D = hidden_states.shape
        T = B * S
        x = hidden_states.reshape(T, D)
        logits = x @ gate_w + gate_b
        probs = jax.nn.softmax(logits.astype(jnp.float32), axis=-1)
        top_w, top_idx = jax.lax.top_k(probs, TOP_K)
        top_w = top_w / jnp.sum(top_w, axis=-1, keepdims=True)
        combine = jnp.zeros((T, NUM_EXPERTS), jnp.float32)
        combine = combine.at[jnp.arange(T)[:, None], top_idx].set(top_w)
        combine = combine.astype(x.dtype)
        h = jax.nn.silu(jnp.einsum('td,edf->tef', x, w1)) * jnp.einsum('td,edf->tef', x, w3)
        out_e = jnp.einsum('tef,efd->ted', h, w2)
        out = jnp.einsum('ted,te->td', out_e, combine)
        return out.reshape(B, S, D)
    x = L0_attn_x
    x = x + _L0_attn_ref(_layernorm(x, axis=-1), L0_attn_wq, L0_attn_wk, L0_attn_wv, L0_attn_wo, L0_attn_bo, L0_attn_cw1, L0_attn_cb1, L0_attn_cw2, L0_attn_cb2, L0_attn_cw3, L0_attn_cb3)
    x = x + _L0_ffn_ref(_layernorm(x, axis=-1), L0_ffn_gate_w, L0_ffn_gate_b, L0_ffn_w1, L0_ffn_w3, L0_ffn_w2)
    return x

_drawn_inputs = setup_inputs


def setup_inputs(seed=0):
    import zlib

    import numpy as np

    out = dict(_drawn_inputs(seed))
    spreads = {}
    factors = {'L0_attn_wq': 8.0,
     'L0_attn_wk': 8.0,
     'L0_attn_wv': 2.694,
     'L0_attn_cw1': 64.0,
     'L0_attn_cb1': 64.0,
     'L0_attn_cw2': 64.0,
     'L0_attn_cb2': 64.0,
     'L0_attn_cw3': 64.0,
     'L0_ffn_gate_b': 3.245,
     'L0_attn_cb3': 8.0}
    for name, (base, spread) in spreads.items():
        noise = np.random.default_rng([zlib.crc32(name.encode()), seed]).standard_normal(out[name].shape)
        drawn = base * np.exp(spread * noise) if base else spread * noise
        out[name] = jnp.asarray(drawn.astype(out[name].dtype))
    for name, factor in factors.items():
        out[name] = (out[name] * factor).astype(out[name].dtype)
    return out
```

```python
import numpy as np
from contextlib import ExitStack

import concourse.bass as bass
from concourse import mybir

P = 128
F32 = mybir.dt.float32
I32 = mybir.dt.int32
ALU = mybir.AluOpType
ACT = mybir.ActivationFunctionType
AX = mybir.AxisListType

H = 16
DH = P // H
WIN = 7
PAD = WIN // 2
WH = WIN * H
EPS = 1e-5


def build(nc, x, wqT, wkT, wvT, woT, bo, conn_in, gate_w, gate_b, w1, w3, w2, ident_in, heads_in, spread_in, out):
    B, L, D = x.shape
    T = B * L
    E, _, F = w1.shape
    FC = F // P
    CH = 512
    NT = CH // P
    NC = T // CH
    CPS = L // CH
    TILES = T // P
    CI = 32
    assert D == P and L % CH == 0

    x_rows = x.rearrange("b l d -> (b l) d").rearrange("(n p) d -> p n d", p=P)
    out_rows = out.rearrange("b l d -> (b l) d").rearrange("(n p) d -> p n d", p=P)

    with ExitStack() as ctx:
        def sb(name, shape, dt=F32):
            return ctx.enter_context(nc.sbuf_tensor(name, shape, dt))

        def bank(name):
            return ctx.enter_context(nc.psum_tensor(name, [P, 512], F32))

        def sem(name):
            return ctx.enter_context(nc.semaphore(name))

        x_tok = sb("x_tok", [P, TILES, D])
        keysT = sb("keysT", [P, B, L + 2 * PAD])
        valsT = sb("valsT", [P, B, L + 2 * PAD])
        queriesT = sb("queriesT", [P, T])
        w1_sb = sb("w1_sb", [P, E, F])
        w3_sb = sb("w3_sb", [P, E, F])
        w2_sb = sb("w2_sb", [P, E, FC, D])
        wq_sb = sb("wq_sb", [P, D])
        wk_sb = sb("wk_sb", [P, D])
        wv_sb = sb("wv_sb", [P, D])
        wo_sb = sb("wo_sb", [P, D])
        bo_sb = sb("bo_sb", [P, D])
        gw_sb = sb("gw_sb", [P, E])
        gb_sb = sb("gb_sb", [P, E])
        ident = sb("ident", [P, P])
        heads = sb("heads", [P, H])
        spread = sb("spread", [WH, WIN, P])
        NCI = conn_in.shape[1]
        conn_p = sb("conn_p", [WH, NCI])
        neg_half = sb("neg_half", [P, NT])

        stats = sb("stats", [P, NT, 6])
        mean_var1 = sb("mean_var1", [P, 2, NT, 2])
        mean_var2 = sb("mean_var2", [P, 2, NT, 2])
        rstd1 = sb("rstd1", [P, NT])
        nmean1 = sb("nmean1", [P, NT])
        xn = sb("xn", [P, 2, NT, D])
        xnT = sb("xnT", [P, 2, CH])
        prod = sb("prod", [P, 3, CH])
        top_score = sb("top_score", [P, NT, H])
        shifted = sb("shifted", [P, NT, WH])
        expd = sb("expd", [P, NT, WH])
        weighted = sb("weighted", [P, NT, WH])
        sum_exp = sb("sum_exp", [P, NT, H])
        sum_wgt = sb("sum_wgt", [P, NT, H])
        denom = sb("denom", [P, NT, H])
        inv_den = sb("inv_den", [P, NT, H])
        fw = sb("fw", [P, NT, WH])
        fwT = sb("fwT", [WH, CH])
        pv = sb("pv", [P, 3, CH])
        x2n = sb("x2n", [P, 2, NT, D])
        x2nT = sb("x2nT", [P, T])
        conn = sb("conn", [P, WH])
        c_h1 = sb("c_h1", [WH, CI])
        c_pre = sb("c_pre", [WH, CI, CI])
        c_h2 = sb("c_h2", [WH, CI])
        c_out = sb("c_out", [WH, 1])
        c_rep = sb("c_rep", [WH, P])
        c_row = sb("c_row", [P, WH])
        c_max = sb("c_max", [P, H])
        c_sum = sb("c_sum", [P, H])
        logit = sb("logit", [P, TILES, E])
        probs = sb("probs", [P, TILES, E])
        combine = sb("combine", [P, TILES, E])
        best = sb("best", [P, TILES, 8])
        rw = sb("rw", [P, TILES])
        hid = sb("hid", [P, 2, FC, CH])
        sil = sb("sil", [P, 2, CH])

        ps_tr = bank("ps_tr")
        ps_fw = bank("ps_fw")
        ps_proj = [bank(f"ps_proj{i}") for i in range(2)]
        ps_score = bank("ps_score")
        ps_exp = [bank(f"ps_exp{i}") for i in range(2)]
        ps_att = bank("ps_att")

        x_loaded = [sem(f"x_loaded{b}") for b in range(B)]
        small_loaded = sem("small_loaded")
        ffn_loaded = sem("ffn_loaded")
        pads_zero = sem("pads_zero")
        consts_set = sem("consts_set")
        dve_done = sem("dve_done")
        pool_done = sem("pool_done")
        conn_ready = sem("conn_ready")
        conn_act = sem("conn_act")
        conn_dve = sem("conn_dve")
        conn_rows = sem("conn_rows")
        ln1_stats = sem("ln1_stats")
        xn_ready = sem("xn_ready")
        x_turned = sem("x_turned")
        xnT_ready = sem("xnT_ready")
        projected = sem("projected")
        qkv_ready = sem("qkv_ready")
        qk_ready = sem("qk_ready")
        scored = sem("scored")
        scores_shifted = sem("scores_shifted")
        exp_ready = sem("exp_ready")
        weighted_ready = sem("weighted_ready")
        fw_ready = sem("fw_ready")
        fw_turned = sem("fw_turned")
        fwT_ready = sem("fwT_ready")
        spread_done = sem("spread_done")
        pv_ready = sem("pv_ready")
        wo_done = sem("wo_done")
        bias_added = sem("bias_added")
        x2_ready = sem("x2_ready")
        ln2_stats = sem("ln2_stats")
        x2n_ready = sem("x2n_ready")
        x2_turned = sem("x2_turned")
        x2nT_ready = sem("x2nT_ready")
        logits_done = sem("logits_done")
        logit_exp = sem("logit_exp")
        logit_shift = sem("logit_shift")
        combine_ready = sem("combine_ready")
        up_done = sem("up_done")
        gated = sem("gated")
        hid_ready = sem("hid_ready")
        down_done = sem("down_done")
        added = sem("added")
        stored = sem("stored")

        small = [(wq_sb[:], wqT), (wk_sb[:], wkT), (wv_sb[:], wvT), (ident[:], ident_in), (heads[:], heads_in),
                 (conn_p[:], conn_in), (spread[:], spread_in), (wo_sb[:], woT), (bo_sb[:], bo), (gw_sb[:], gate_w),
                 (gb_sb[:], gate_b)]
        SMALL = 16 * len(small)
        FFN_LOADS = 16 * 3
        STEPS = range(-4, NC + 1)

        block = ctx.enter_context(nc.Block())

        def steps(stages):
            for i in STEPS:
                for lead, stage in stages:
                    if 0 <= i + lead < NC:
                        stage(i + lead)

        def cols(c):
            return c // CPS, (c % CPS) * CH

        @block.sync
        def _(sp):
            half = TILES // B
            for b in range(B):
                sp.dma_start(x_tok[:, b * half:(b + 1) * half, :], x_rows[:, b * half:(b + 1) * half, :]).then_inc(x_loaded[b], 16)
            sp.dma_start(w1_sb[:], w1.rearrange("e d f -> d e f")).then_inc(ffn_loaded, 16)
            sp.dma_start(w3_sb[:], w3.rearrange("e d f -> d e f")).then_inc(ffn_loaded, 16)
            sp.dma_start(w2_sb[:], w2.rearrange("e (j p) d -> p e j d", p=P)).then_inc(ffn_loaded, 16)
            for c in range(NC):
                sp.wait_ge(added, NT * ((E - 1) * NC + c + 1))
                sp.dma_start(out_rows[:, c * NT:(c + 1) * NT, :], x_tok[:, c * NT:(c + 1) * NT, :]).then_inc(stored, 16)
            sp.wait_ge(stored, 16 * NC)

        @block.gpsimd
        def _(pool):
            nc.gpsimd.memset(neg_half[:], -0.5)
            for t in (keysT, valsT):
                nc.gpsimd.memset(t[:, :, 0:PAD], 0.0)
                last = nc.gpsimd.memset(t[:, :, L + PAD:], 0.0)
            last.then_inc(pads_zero, 1)
            pool.wait_ge(pads_zero, 1)
            chain = [0]

            def link(ins):
                chain[0] += 1
                ins.then_inc(pool_done, 1)
                pool.wait_ge(pool_done, chain[0])

            def normalise(mv, src, dst, ready):
                link(nc.gpsimd.tensor_scalar(rstd1[:], mv[:, :, 1], EPS, None, ALU.add))
                nc.gpsimd.tensor_scalar(nmean1[:], mv[:, :, 0], -1.0, None, ALU.mult)
                link(nc.gpsimd.tensor_tensor(rstd1[:], rstd1[:], neg_half[:], ALU.pow))
                for t in range(NT):
                    last = nc.gpsimd.tensor_scalar(dst[:, t, :], src[:, t, :], nmean1[:, t:t + 1], rstd1[:, t:t + 1],
                                                   ALU.add, ALU.mult)
                last.then_inc(ready, 1)

            def weigh(c):
                if c == 0:
                    pool.wait_ge(conn_ready, 1)
                pool.wait_ge(exp_ready, c + 1)
                if c >= 1:
                    pool.wait_ge(fw_ready, c)
                nc.gpsimd.tensor_tensor(weighted[:], expd[:], conn[:].rearrange("p (a n) -> p a n", a=1).to_broadcast([P, NT, WH]),
                                        ALU.mult).then_inc(weighted_ready, 1)

            def ln1(c):
                pool.wait_ge(ln1_stats, c + 1)
                if c >= 2:
                    pool.wait_ge(x_turned, c - 1)
                normalise(mean_var1[:, c % 2], x_tok[:, c * NT:(c + 1) * NT, :], xn[:, c % 2], xn_ready)

            def add_bias(c):
                if c == 0:
                    pool.wait_ge(small_loaded, SMALL)
                pool.wait_ge(xn_ready, c + 1)
                nc.gpsimd.tensor_tensor(x_tok[:, c * NT:(c + 1) * NT, :], x_tok[:, c * NT:(c + 1) * NT, :],
                                        bo_sb[:].rearrange("p (a n) -> p a n", a=1).to_broadcast([P, NT, D]), ALU.add).then_inc(bias_added, 1)

            def ln2(c):
                pool.wait_ge(ln2_stats, c + 1)
                if c >= 2:
                    pool.wait_ge(x2_turned, c - 1)
                normalise(mean_var2[:, c % 2], x_tok[:, c * NT:(c + 1) * NT, :], x2n[:, c % 2], x2n_ready)

            steps([(0, weigh), (4, ln1), (4, add_bias), (0, ln2)])

        @block.scalar
        def _(act):
            for dst, src in small:
                act.dma_start(dst, src).then_inc(small_loaded, 16)
            act.wait_ge(conn_dve, 1)
            nc.scalar.activation(c_h1[:], c_h1[:], ACT.Gelu).then_inc(conn_act, 1)
            act.wait_ge(conn_dve, 2)
            nc.scalar.activation(c_h2[:], c_h2[:], ACT.Gelu).then_inc(conn_act, 1)
            act.wait_ge(conn_dve, 4)
            nc.scalar.activation(c_row[:], c_row[:], ACT.Exp).then_inc(conn_act, 1)

            def xnT_out(c):
                act.wait_ge(x_turned, c + 1)
                if c >= 2:
                    act.wait_ge(projected, 3 * (c - 1))
                nc.scalar.copy(xnT[:, c % 2, :], ps_tr[:]).then_inc(xnT_ready, 1)

            def qkv_out(c):
                b, o = cols(c)
                if c == 0:
                    act.wait_ge(pads_zero, 1)
                dst = [queriesT[:, c * CH:(c + 1) * CH], keysT[:, b, PAD + o:PAD + o + CH], valsT[:, b, PAD + o:PAD + o + CH]]
                for j in range(3):
                    act.wait_ge(projected, 3 * c + j + 1)
                    nc.scalar.copy(dst[j], ps_proj[(3 * c + j) % 2][:]).then_inc(qkv_ready, 1)

            def exp(c):
                act.wait_ge(scores_shifted, c + 1)
                if c >= 1:
                    act.wait_ge(fw_ready, c)
                nc.scalar.activation(expd[:], shifted[:], ACT.Exp, scale=float(1.0 / np.sqrt(np.float32(DH)))).then_inc(exp_ready, 1)

            def fwT_out(c):
                act.wait_ge(fw_turned, c + 1)
                if c >= 1:
                    act.wait_ge(spread_done, WIN * c)
                nc.scalar.copy(fwT[:], ps_fw[0:WH, :]).then_inc(fwT_ready, 1)

            def x2nT_out(c):
                act.wait_ge(x2_turned, c + 1)
                nc.scalar.copy(x2nT[:, c * CH:(c + 1) * CH], ps_fw[:]).then_inc(x2nT_ready, 1)

            steps([(0, exp), (2, qkv_out), (3, xnT_out), (-1, x2nT_out), (0, fwT_out)])

            act.wait_ge(logit_shift, 1)
            nc.scalar.activation(probs[:], logit[:], ACT.Exp).then_inc(logit_exp, 1)

            for n in range(E * NC * FC):
                act.wait_ge(up_done, n + 1)
                if n >= 2:
                    act.wait_ge(hid_ready, n - 1)
                nc.scalar.activation(sil[:, n % 2, :], [ps_tr, ps_fw][n % 2][:], ACT.Silu).then_inc(gated, 1)

        @block.vector
        def _(dve):
            chain = [0]

            def link(ins):
                chain[0] += 1
                ins.then_inc(dve_done, 1)
                dve.wait_ge(dve_done, chain[0])

            dve.wait_ge(small_loaded, SMALL)
            at = 0

            def part(n):
                nonlocal at
                at += n
                return conn_p[:, at - n:at]

            cw1, cb1, cw2, cb2, cw3, cb3, pos = [part(n) for n in (CI, CI, CI * CI, CI, CI, 1, 1)]
            nc.vector.scalar_tensor_tensor(out=c_h1[:], in0=cw1, scalar=pos, in1=cb1, op0=ALU.mult, op1=ALU.add).then_inc(conn_dve, 1)
            dve.wait_ge(conn_act, 1)
            link(nc.vector.tensor_tensor(c_pre[:], cw2.rearrange("p (j i) -> p j i", i=CI),
                                         c_h1[:].rearrange("p (a i) -> p a i", a=1).to_broadcast([WH, CI, CI]), ALU.mult))
            link(nc.vector.tensor_reduce(c_h2[:], c_pre[:], AX.X, ALU.add))
            nc.vector.tensor_tensor(c_h2[:], c_h2[:], cb2, ALU.add).then_inc(conn_dve, 1)
            dve.wait_ge(conn_act, 2)
            link(nc.vector.tensor_tensor(c_h2[:], c_h2[:], cw3, ALU.mult))
            link(nc.vector.tensor_reduce(c_out[:], c_h2[:], AX.X, ALU.add))
            link(nc.vector.tensor_tensor(c_out[:], c_out[:], cb3, ALU.add))
            nc.vector.tensor_copy(c_rep[:], c_out[:].to_broadcast([WH, P])).then_inc(conn_dve, 1)
            dve.wait_ge(conn_rows, 1)
            by_head = "p (w h) -> p h w"
            link(nc.vector.tensor_reduce(c_max[:], ps_score[:, 0:WH].rearrange(by_head, h=H), AX.X, ALU.max))
            nc.vector.tensor_tensor(c_row[:].rearrange("p (w h) -> p w h", h=H), ps_score[:, 0:WH].rearrange("p (w h) -> p w h", h=H),
                                    c_max[:].rearrange("p (a h) -> p a h", a=1).to_broadcast([P, WIN, H]), ALU.subtract).then_inc(conn_dve, 1)
            dve.wait_ge(conn_act, 3)
            link(nc.vector.tensor_reduce(c_sum[:], c_row[:].rearrange(by_head, h=H), AX.X, ALU.add))
            link(nc.vector.reciprocal(c_sum[:], c_sum[:]))
            nc.vector.tensor_tensor(conn[:].rearrange("p (w h) -> p w h", h=H), c_row[:].rearrange("p (w h) -> p w h", h=H),
                                    c_sum[:].rearrange("p (a h) -> p a h", a=1).to_broadcast([P, WIN, H]), ALU.mult).then_inc(conn_ready, 1)

            def moments(src, mv, ready):
                for t in range(NT):
                    last = nc.vector.bn_stats(stats[:, t, :], src[:, t, :])
                link(last)
                for t in range(NT):
                    last = nc.vector.bn_aggr(mv[:, t, :], stats[:, t, :])
                link(last)
                nc.vector.engine_nop().then_inc(ready, 1)

            def ln1(c):
                if c % CPS == 0:
                    dve.wait_ge(x_loaded[c // CPS], 16)
                if c >= 2:
                    dve.wait_ge(xn_ready, c - 1)
                moments(x_tok[:, c * NT:(c + 1) * NT, :], mean_var1[:, c % 2], ln1_stats)

            def qk(c):
                b, o = cols(c)
                dve.wait_ge(qkv_ready, 3 * (c + 2 if c % CPS < CPS - 1 else c + 1))
                for w in range(WIN):
                    n = WIN * c + w
                    if n >= 3:
                        dve.wait_ge(scored, n - 2)
                    nc.vector.tensor_tensor(prod[:, n % 3, :], queriesT[:, c * CH:(c + 1) * CH],
                                            keysT[:, b, o + w:o + w + CH], ALU.mult).then_inc(qk_ready, 1)

            s_whn = ps_score[:, 0:NT * WH]

            def per_head(t):
                return t.rearrange("p t (a h) -> p t a h", a=1).to_broadcast([P, NT, WIN, H])

            def softmax_a(c):
                dve.wait_ge(scored, WIN * (c + 1))
                link(nc.vector.tensor_reduce(top_score[:], s_whn.rearrange("p (t w h) -> p t h w", t=NT, w=WIN), AX.X, ALU.max))
                if c >= 1:
                    dve.wait_ge(exp_ready, c)
                nc.vector.tensor_tensor(shifted[:].rearrange("p t (w h) -> p t w h", h=H),
                                        s_whn.rearrange("p (t w h) -> p t w h", t=NT, w=WIN),
                                        per_head(top_score[:]), ALU.subtract).then_inc(scores_shifted, 1)

            def softmax_b(c):
                dve.wait_ge(exp_ready, c + 1)
                nc.vector.tensor_reduce(sum_exp[:], expd[:].rearrange("p t (w h) -> p t h w", h=H), AX.X, ALU.add)
                dve.wait_ge(weighted_ready, c + 1)
                link(nc.vector.tensor_reduce(sum_wgt[:], weighted[:].rearrange("p t (w h) -> p t h w", h=H), AX.X, ALU.add))
                link(nc.vector.scalar_tensor_tensor(out=denom[:], in0=sum_exp[:], scalar=1e-9, in1=sum_wgt[:],
                                                    op0=ALU.mult, op1=ALU.add))
                link(nc.vector.reciprocal(inv_den[:], denom[:]))
                if c >= 1:
                    dve.wait_ge(fw_turned, c)
                nc.vector.tensor_tensor(fw[:].rearrange("p t (w h) -> p t w h", h=H),
                                        weighted[:].rearrange("p t (w h) -> p t w h", h=H),
                                        per_head(inv_den[:]), ALU.mult).then_inc(fw_ready, 1)

            def pvs(c):
                b, o = cols(c)
                for w in range(WIN):
                    n = WIN * c + w
                    dve.wait_ge(spread_done, n + 1)
                    if n >= 3:
                        dve.wait_ge(wo_done, n - 2)
                    nc.vector.tensor_tensor(pv[:, n % 3, :], ps_exp[n % 2][:], valsT[:, b, o + w:o + w + CH],
                                            ALU.mult).then_inc(pv_ready, 1)

            def residual(c):
                dve.wait_ge(wo_done, WIN * (c + 1))
                dve.wait_ge(bias_added, c + 1)
                xs = x_tok[:, c * NT:(c + 1) * NT, :]
                nc.vector.tensor_tensor(xs, ps_att[:].rearrange("p (t d) -> p t d", t=NT), xs, ALU.add).then_inc(x2_ready, 1)
                dve.wait_ge(x2_ready, c + 1)
                if c >= 2:
                    dve.wait_ge(x2n_ready, c - 1)
                moments(xs, mean_var2[:, c % 2], ln2_stats)

            steps([(0, softmax_a), (1, qk), (0, softmax_b), (4, ln1), (0, pvs), (0, residual)])

            def per_token(t):
                return t.rearrange("p (t a) -> p t a", a=1).to_broadcast([P, TILES, E])

            dve.wait_ge(logits_done, 1)
            link(nc.vector.tensor_tensor(logit[:], ps_score[:, 0:TILES * E].rearrange("p (t e) -> p t e", e=E),
                                         gb_sb[:].rearrange("p (a e) -> p a e", a=1).to_broadcast([P, TILES, E]), ALU.add))
            link(nc.vector.tensor_reduce(rw[:], logit[:], AX.X, ALU.max))
            nc.vector.tensor_tensor(logit[:], logit[:], per_token(rw[:]), ALU.subtract).then_inc(logit_shift, 1)
            dve.wait_ge(logit_exp, 1)
            for t in range(TILES):
                last = nc.vector.max(best[:, t, :], probs[:, t, :])
            link(last)
            link(nc.vector.tensor_tensor(combine[:], probs[:], per_token(best[:, :, 1]), ALU.is_ge))
            link(nc.vector.tensor_tensor(combine[:], combine[:], probs[:], ALU.mult))
            link(nc.vector.tensor_tensor(rw[:], best[:, :, 0], best[:, :, 1], ALU.add))
            link(nc.vector.reciprocal(rw[:], rw[:]))
            link(nc.vector.tensor_tensor(combine[:], combine[:], per_token(rw[:]), ALU.mult))

            def gather_down(k):
                e, c = divmod(k, NC)
                for t in range(NT):
                    tile = c * NT + t
                    dve.wait_ge(down_done, NT * k + t + 1)
                    if e:
                        dve.wait_ge(added, NT * ((e - 1) * NC + c) + t + 1)
                    nc.vector.scalar_tensor_tensor(out=x_tok[:, tile, :], in0=[ps_score, ps_att][t % 2][:, 0:D],
                                                   scalar=combine[:, tile, e:e + 1], in1=x_tok[:, tile, :],
                                                   op0=ALU.mult, op1=ALU.add).then_inc(added, 1)

            for k in range(E * NC):
                for j in range(FC):
                    n = k * FC + j
                    dve.wait_ge(gated, n + 1)
                    if k >= 2:
                        dve.wait_ge(down_done, NT * (k - 1))
                    nc.vector.tensor_tensor(hid[:, k % 2, j, :], sil[:, n % 2, :], ps_proj[n % 2][:], ALU.mult).then_inc(hid_ready, 1)
                if k:
                    gather_down(k - 1)
            gather_down(E * NC - 1)

        @block.tensor
        def _(pe):
            pe.wait_ge(small_loaded, SMALL)
            pe.wait_ge(conn_dve, 3)
            nc.tensor.matmul(ps_score[:, 0:WH], c_rep[:], ident[0:WH, 0:WH], start=True, stop=True).then_inc(conn_rows, 1)

            def turn(c):
                pe.wait_ge(xn_ready, c + 1)
                if c:
                    pe.wait_ge(xnT_ready, c)
                for t in range(NT):
                    last = nc.tensor.transpose(ps_tr[:, t * P:(t + 1) * P], xn[:, c % 2, t, :], ident[:])
                last.then_inc(x_turned, 1)

            def project(c):
                pe.wait_ge(xnT_ready, c + 1)
                for j, w in enumerate((wq_sb, wk_sb, wv_sb)):
                    n = 3 * c + j
                    if n >= 2:
                        pe.wait_ge(qkv_ready, n - 1)
                    nc.tensor.matmul(ps_proj[n % 2][:], w[:], xnT[:, c % 2, :], start=True, stop=True).then_inc(projected, 1)

            def score(c):
                if c == 0:
                    pe.wait_ge(conn_ready, 1)
                else:
                    pe.wait_ge(scores_shifted, c)
                for w in range(WIN):
                    n = WIN * c + w
                    pe.wait_ge(qk_ready, n + 1)
                    for t in range(NT):
                        at = t * WH + w * H
                        last = nc.tensor.matmul(ps_score[:, at:at + H], prod[:, n % 3, t * P:(t + 1) * P], heads[:],
                                                start=True, stop=True)
                    last.then_inc(scored, 1)

            def turn2(c):
                pe.wait_ge(x2n_ready, c + 1)
                pe.wait_ge(fwT_ready, c + 1)
                for t in range(NT):
                    last = nc.tensor.transpose(ps_fw[:, t * P:(t + 1) * P], x2n[:, c % 2, t, :], ident[:])
                last.then_inc(x2_turned, 1)

            def turn_fw(c):
                pe.wait_ge(fw_ready, c + 1)
                if c:
                    pe.wait_ge(x2nT_ready, c)
                for t in range(NT):
                    last = nc.tensor.transpose(ps_fw[0:WH, t * P:(t + 1) * P], fw[:, t, :], ident[:])
                last.then_inc(fw_turned, 1)

            def attend(c):
                pe.wait_ge(fwT_ready, c + 1)

                def spread_w(w):
                    n = WIN * c + w
                    if n >= 2:
                        pe.wait_ge(pv_ready, n - 1)
                    nc.tensor.matmul(ps_exp[n % 2][:], spread[:, w, :], fwT[:], start=True, stop=True).then_inc(spread_done, 1)

                def out_w(w):
                    n = WIN * c + w
                    pe.wait_ge(pv_ready, n + 1)
                    if w == 0 and c:
                        pe.wait_ge(x2_ready, c)
                    for t in range(NT):
                        last = nc.tensor.matmul(ps_att[:, t * D:(t + 1) * D], pv[:, n % 3, t * P:(t + 1) * P], wo_sb[:],
                                                start=(w == 0 and t == 0), stop=(w == WIN - 1 and t == NT - 1),
                                                skip_group_check=True)
                    last.then_inc(wo_done, 1)

                spread_w(0)
                for w in range(1, WIN):
                    spread_w(w)
                    out_w(w - 1)
                out_w(WIN - 1)

            steps([(2, project), (3, turn), (1, score), (-1, turn2), (0, turn_fw), (0, attend)])

            pe.wait_ge(x2nT_ready, NC)
            pe.wait_ge(scores_shifted, NC)
            for t in range(TILES):
                last = nc.tensor.matmul(ps_score[:, t * E:(t + 1) * E], x2nT[:, t * P:(t + 1) * P], gw_sb[:], start=True, stop=True)
            last.then_inc(logits_done, 1)

            pe.wait_ge(ffn_loaded, FFN_LOADS)
            pe.wait_ge(logit_shift, 1)
            pe.wait_ge(x2_ready, NC)

            def up(k):
                e, c = divmod(k, NC)
                for j in range(FC):
                    n = k * FC + j
                    if n >= 2:
                        pe.wait_ge(hid_ready, n - 1)
                    rhs = x2nT[:, c * CH:(c + 1) * CH]
                    nc.tensor.matmul([ps_tr, ps_fw][n % 2][:], w1_sb[:, e, j * P:(j + 1) * P], rhs, start=True, stop=True)
                    nc.tensor.matmul(ps_proj[n % 2][:], w3_sb[:, e, j * P:(j + 1) * P], rhs, start=True, stop=True).then_inc(up_done, 1)

            def down(k):
                e = k // NC
                pe.wait_ge(hid_ready, FC * (k + 1))
                for t in range(NT):
                    m = NT * k + t
                    if m >= 2:
                        pe.wait_ge(added, m - 1)
                    for j in range(FC):
                        last = nc.tensor.matmul([ps_score, ps_att][t % 2][:, 0:D], hid[:, k % 2, j, t * P:(t + 1) * P],
                                                w2_sb[:, e, j, :], start=(j == 0), stop=(j == FC - 1))
                    last.then_inc(down_done, 1)

            for k in range(E * NC):
                up(k)
                if k:
                    down(k - 1)
            down(E * NC - 1)


def kernel(**inputs):
    import concourse.bacc as bacc
    from concourse.bass_utils import run_bass_kernel_spmd

    g = {k: np.asarray(v) for k, v in inputs.items()}
    a = {k[8:]: v for k, v in g.items() if k.startswith("L0_attn_")}
    f = {k[7:]: v for k, v in g.items() if k.startswith("L0_ffn_")}

    def rows(v):
        return np.ascontiguousarray(np.broadcast_to(v.reshape(1, -1), (P, v.size)))

    def per_place(v):
        v = v.reshape(H, -1)
        return np.broadcast_to(v[None], (WIN,) + v.shape).reshape(WH, -1)

    pos = np.repeat(np.linspace(0.0, 1.0, WIN, dtype=np.float32), H)[:, None]
    ident = np.eye(P, dtype=np.float32)
    heads = np.repeat(np.eye(H, dtype=np.float32), DH, axis=0)
    spread = np.zeros((WIN, H, WIN, P), np.float32)
    for w in range(WIN):
        spread[w, :, w, :] = heads.T
    arrays = {
        "x": a["x"], "wqT": a["wq"].T, "wkT": a["wk"].T, "wvT": a["wv"].T, "woT": a["wo"].T, "bo": rows(a["bo"]),
        "conn": np.concatenate([per_place(a[k]) for k in ("cw1", "cb1", "cw2", "cb2", "cw3", "cb3")] + [pos], axis=1),
        "gate_w": f["gate_w"], "gate_b": rows(f["gate_b"]), "w1": f["w1"], "w3": f["w3"], "w2": f["w2"],
        "ident": ident, "heads": heads, "spread": spread.reshape(WH, WIN, P),
    }
    arrays = {k: np.ascontiguousarray(v) for k, v in arrays.items()}
    nc = bacc.Bacc("TRN2", target_bir_lowering=False, num_devices=1)
    args = [nc.dram_tensor(f"in_{k}", v.shape, mybir.dt.from_np(v.dtype), kind="ExternalInput").ap() for k, v in arrays.items()]
    out = nc.dram_tensor("out_y", a["x"].shape, F32, kind="ExternalOutput").ap()
    build(nc, *args, out)
    r = run_bass_kernel_spmd(nc, [{f"in_{k}": v for k, v in arrays.items()}], core_ids=[0])
    return r.results[0]["out_y"]
```

```python
import numpy as np
from contextlib import ExitStack

import concourse.bass as bass
from concourse import mybir

P = 128
F32 = mybir.dt.float32
F32R = mybir.dt.float32r
BF16 = mybir.dt.bfloat16
I32 = mybir.dt.int32
U32 = mybir.dt.uint32
ALU = mybir.AluOpType
ACT = mybir.ActivationFunctionType
AX = mybir.AxisListType

H = 16
DH = P // H
WIN = 7
PAD = WIN // 2
WH = WIN * H
EPS = 1e-5
RING = 8


def build(nc, x, wqT, wkT, wvT, woT, bo, conn_in, gate_w, gate_b, w1, w3, w2, ident_in, heads_in, spread_in, iota_in, count_in, reset_in, out):
    B, L, D = x.shape
    T = B * L
    E, _, F = w1.shape
    FC = F // P
    CH = 512
    NT = CH // P
    NC = T // CH
    CPS = L // CH
    TILES = T // P
    CI = 32
    assert D == P and L % CH == 0

    x_rows = x.rearrange("b l d -> (b l) d").rearrange("(n p) d -> p n d", p=P)
    out_rows = out.rearrange("(n p) d -> p n d", p=P)
    K = 2
    SLOTS = -(-(K * T // P + E - 1) // RING) * RING
    ROW = D + K
    token_rows = nc.dram_tensor("token_rows", (T + P, ROW), F32).ap()
    token_tiles = token_rows.rearrange("(n p) d -> p n d", p=P)

    with ExitStack() as ctx:
        def sb(name, shape, dt=F32):
            return ctx.enter_context(nc.sbuf_tensor(name, shape, dt))

        def bank(name):
            return ctx.enter_context(nc.psum_tensor(name, [P, 512], F32))

        def sem(name):
            return ctx.enter_context(nc.semaphore(name))

        x_tok = sb("x_tok", [P, TILES, D])
        KV = B * (L + 2 * PAD)
        attn_mem = sb("attn_mem", [P, 2 * KV + 3 * CH])
        keysT, valsT = (attn_mem[:, j * KV:(j + 1) * KV].rearrange("p (b l) -> p b l", b=B) for j in range(2))
        queriesT = attn_mem[:, 2 * KV:].rearrange("p (r n) -> p r n", r=3)
        w_hi = sb("w_hi", [P, K, E, F], F32R)
        w_lo = sb("w_lo", [P, K, E, F], F32R)
        w2_sb = sb("w2_sb", [P, E, FC, D])
        wq_sb = sb("wq_sb", [P, D])
        wk_sb = sb("wk_sb", [P, D])
        wv_sb = sb("wv_sb", [P, D])
        wo_sb = sb("wo_sb", [P, D])
        bo_sb = sb("bo_sb", [P, D])
        gw_sb = sb("gw_sb", [P, E])
        gb_sb = sb("gb_sb", [P, E])
        def share(t, shapes):
            flat, at, views = t[:], 0, []
            for parts, *dims in shapes:
                n = int(np.prod(dims))
                names = "abc"[:len(dims)]
                v = flat[0:parts, at:at + n]
                if len(dims) > 1:
                    v = v.rearrange(f"p ({' '.join(names)}) -> p {' '.join(names)}", **dict(zip(names[1:], dims[1:])))
                views.append(v)
                at += n
            return views

        NCI = conn_in.shape[1]
        w_raw_mem = sb("w_raw_mem", [P, 4 * F])
        w_raw, = share(w_raw_mem, [(P, 4, F)])
        conn_p, count_w = share(w_raw_mem, [(WH, NCI), (P, 2, P)])
        products = sb("products", [P, 3 * CH])
        prod, = share(products, [(P, 3, CH)])
        upto, ahead, passed, empty, from_tile, from_part, second, token = share(
            products, [(P, E, TILES), (P, E, TILES), (1, SLOTS, E)] + [(P, SLOTS)] * 5)
        values = sb("values", [P, 4 * CH])
        pv, = share(values, [(P, 4, CH)])
        y = share(values, [(P, D)] * RING)
        xn_mem = sb("xn_mem", [P, max(2 * NT * D, RING * ROW)])
        xn, = share(xn_mem, [(P, 2, NT, D)])
        xg = share(xn_mem, [(P, ROW)] * RING)
        soft_a, soft_b = (sb(f"soft_{n}", [P, 2 * F]) for n in "ab")
        sil, = share(soft_a, [(P, 2, F)])
        shifted, expd = share(soft_a, [(P, NT, WH)] * 2)
        spread_raw, = share(soft_a, [(WH, WIN, P)])
        hid, = share(soft_b, [(P, 2, F)])
        weighted, fw = share(soft_b, [(P, NT, WH)] * 2)
        place_of_mem, = share(soft_b, [(P, K * E, TILES)])
        place_of = place_of_mem.rearrange("p (k e) t -> p k e t", k=K)
        ident = sb("ident", [P, P])
        heads = sb("heads", [P, (2 * WIN - 1) * H])
        hidT = sb("hidT", [P, 2, F])
        scoresT = hidT[0:WH, 0, :]
        spread = sb("spread", [WH, WIN, P], F32R)
        neg_half = sb("neg_half", [P, NT])

        stats = sb("stats", [P, NT, 6])
        mean_var1 = sb("mean_var1", [P, 2, NT, 2])
        mean_var2 = sb("mean_var2", [P, 2, NT, 2])
        rstd = sb("rstd", [P, 2, NT])
        nmean = sb("nmean", [P, 2, NT])
        xnT = sb("xnT", [P, 2, CH])
        top_score = sb("top_score", [P, NT, H])
        sum_exp = sb("sum_exp", [P, NT, H])
        sum_wgt = sb("sum_wgt", [P, NT, H])
        denom = sb("denom", [P, NT, H])
        inv_den = sb("inv_den", [P, NT, H])
        hi_mem = sb("hi_mem", [P, CH], F32R)
        lo_mem = sb("lo_mem", [P, CH], F32R)
        fwT_hi, fwT_lo = (t[0:WH, :] for t in (hi_mem, lo_mem))
        x_hi, x_lo = (t[:, 0:2 * P].rearrange("p (r n) -> p r n", r=2) for t in (hi_mem, lo_mem))
        x2n = sb("x2n", [P, 2, NT, ROW])
        x2nT = sb("x2nT", [P, CH])
        conn = sb("conn", [P, WH])
        c_h1 = sb("c_h1", [WH, CI])
        c_pre = hidT[:].rearrange("p a f -> p (a f)")[0:WH, 0:CI * CI].rearrange("p (j i) -> p j i", j=CI)
        c_h2 = sb("c_h2", [WH, CI])
        c_out = sb("c_out", [WH, 1])
        c_rep = sb("c_rep", [WH, P])
        c_row = sb("c_row", [P, WH])
        c_max = sb("c_max", [P, H])
        c_sum = sb("c_sum", [P, H])
        logit = sb("logit", [P, NT, E])
        best = sb("best", [P, NT, 8])
        best_at = sb("best_at", [P, NT, 8], U32)
        gap = sb("gap", [P, 2, NT])
        gap_exp = sb("gap_exp", [P, 2, NT])
        one_plus = sb("one_plus", [P, NT])
        IOTA = iota_in.shape[1]
        iota = sb("iota", [P, IOTA])
        iota16 = sb("iota16", [P, P], BF16)
        own = iota[:, P:P + 1]
        count_w16 = sb("count_w16", [P, 2, P], BF16)
        reset = sb("reset", [P, E, TILES])
        chosen = sb("chosen", [P, K, E, TILES])
        either = sb("either", [P, E, TILES], BF16)
        need_i = sb("need_i", [P, E], I32)
        need = sb("need", [P, E])
        need_upto = sb("need_upto", [P, E])
        begin = sb("begin", [P, E])
        slot = sb("slot", [P, K, TILES])
        slot_i = sb("slot_i", [P, 3, K, TILES], I32)
        slot_tile = sb("slot_tile", [P, K, TILES])
        slot_part = sb("slot_part", [P, K, TILES])
        hots = attn_mem[:].bitcast(BF16)
        PH = K * TILES * P
        part_hot = hots[:, 0:PH].rearrange("p (n c) -> p n c", c=P)
        tile_hot = hots[:, PH:PH + K * TILES * 2 * SLOTS].rearrange("p (n a s) -> p n a s", a=2, s=SLOTS)
        slot_meta = sb("slot_meta", [P, SLOTS, 2], I32)
        expert_f = sb("expert_f", [1, SLOTS])
        expert_of = sb("expert_of", [1, SLOTS], I32)
        zero_rows = sb("zero_rows", [P, ROW])
        meta = [sb(f"meta{r}", [P, 2], I32) for r in range(RING)]
        coef = [sb(f"coef{r}", [P, 1]) for r in range(RING)]

        ps_tr = bank("ps_tr")
        ps_fw = bank("ps_fw")
        ps_proj = [bank(f"ps_proj{i}") for i in range(2)]
        ps_score = bank("ps_score")
        ps_exp = [bank(f"ps_exp{i}") for i in range(2)]
        ps_att = bank("ps_att")

        ps_count = ps_score
        ps_x, ps_hid, ps_y = ps_tr, ps_fw, ps_att
        ps_gate, ps_up = ps_proj, ps_exp

        x_loaded = [sem(f"x_loaded{c}") for c in range(NC)]
        first_loaded = sem("first_loaded")
        conn_loaded = sem("conn_loaded")
        small_loaded = sem("small_loaded")
        ffn_loaded = sem("ffn_loaded")
        pads_zero = sem("pads_zero")
        consts_set = sem("consts_set")
        dve_done = sem("dve_done")
        pool_done = sem("pool_done")
        conn_ready = sem("conn_ready")
        conn_act = sem("conn_act")
        conn_dve = sem("conn_dve")
        conn_rows = sem("conn_rows")
        ln1_stats = sem("ln1_stats")
        xn_ready = sem("xn_ready")
        x_turned = sem("x_turned")
        xnT_ready = sem("xnT_ready")
        projected = sem("projected")
        qkv_ready = sem("qkv_ready")
        qk_ready = sem("qk_ready")
        scored = sem("scored")
        scoresT_ready = sem("scoresT_ready")
        scores_turned = sem("scores_turned")
        scores_shifted = sem("scores_shifted")
        exp_ready = sem("exp_ready")
        weighted_ready = sem("weighted_ready")
        fw_ready = sem("fw_ready")
        fw_turned = sem("fw_turned")
        fwT_hi_ready = sem("fwT_hi_ready")
        fwT_ready = sem("fwT_ready")
        spread_done = sem("spread_done")
        pv_ready = sem("pv_ready")
        pair_ready = sem("pair_ready")
        wo_done = sem("wo_done")
        bias_added = sem("bias_added")
        x2_ready = sem("x2_ready")
        ln2_stats = sem("ln2_stats")
        x2n_ready = sem("x2n_ready")
        x2_turned = sem("x2_turned")
        x2nT_ready = sem("x2nT_ready")
        logits_done = sem("logits_done")
        logits_read = sem("logits_read")
        gap_ready = sem("gap_ready")
        gap_exp_ready = sem("gap_exp_ready")
        weights_ready = sem("weights_ready")
        x2nT_used = sem("x2nT_used")
        w_loaded = [sem(f"w_loaded{i}") for i in range(4)]
        w_hi_ready = sem("w_hi_ready")
        w_split = sem("w_split")
        zero_ready = sem("zero_ready")
        rows_stored = [sem(f"rows_stored{i}") for i in range(2)]
        x2_stored = sem("x2_stored")
        counted = sem("counted")
        hots_ready = sem("hots_ready")
        table_done = sem("table_done")
        table_read = sem("table_read")
        meta_copied = sem("meta_copied")
        gathered = [sem(f"gathered{r}") for r in range(RING)]
        scattered = [sem(f"scattered{r}") for r in range(RING)]
        coef_ready = sem("coef_ready")
        xg_turned = sem("xg_turned")
        x_hi_ready = sem("x_hi_ready")
        xg_split = sem("xg_split")
        gate_done = sem("gate_done")
        up_done = sem("up_done")
        silu_done = sem("silu_done")
        hid_ready = sem("hid_ready")
        hid_turned = sem("hid_turned")
        hidT_ready = sem("hidT_ready")
        down_done = sem("down_done")
        y_ready = sem("y_ready")

        first = [(ident[:], ident_in), (wq_sb[:], wqT), (wk_sb[:], wkT), (wv_sb[:], wvT)]
        conn_first = [(conn_p, conn_in), (heads[:], heads_in)]
        small = [(bo_sb[:], bo), (spread_raw, spread_in), (wo_sb[:], woT), (gw_sb[:], gate_w),
                 (gb_sb[:], gate_b), (iota[:], iota_in), (count_w, count_in), (reset[:], reset_in)]
        FIRST = 16 * len(first)
        CONN = 16 * len(conn_first)
        SMALL = 16 * len(small)
        STEPS = range(-6, NC + 2)

        def tile_steps(eng, first, last, stages):
            leads = [lead for lead, _ in stages]
            lo = -(-(-min(leads)) // RING)
            hi = (SLOTS - max(max(leads), 0)) // RING

            def step(i, u, ends):
                for lead, stage in stages:
                    if not ends or 0 <= RING * i + u + lead < SLOTS:
                        ahead_by, r = divmod(u + lead, RING)
                        stage(RING * i + (u + lead), i + ahead_by, r)

            lo = max(lo, -(-first // RING), 1)
            for s in range(first, RING * lo):
                step(s // RING, s % RING, True)
            with eng.Fori(lo, hi) as i:
                for u in range(RING):
                    step(i, u, False)
            for s in range(RING * hi, last + 1):
                step(s // RING, s % RING, True)

        block = ctx.enter_context(nc.Block())

        QLEAD = 1

        def on(stage, c, *w):
            if 0 <= c < NC:
                stage(c, *w)

        UNITS = (WIN + 1) // 2

        def cols(c):
            return c // CPS, (c % CPS) * CH

        @block.sync
        def _(sp):
            for c in range(NC):
                sp.dma_start(x_tok[:, c * NT:(c + 1) * NT, :], x_rows[:, c * NT:(c + 1) * NT, :]).then_inc(x_loaded[c], 16)
            def load_w(n):
                if n >= 4:
                    sp.wait_ge(w_split, n - 3)
                sp.dma_start(w_raw[:, n % 4, :], (w1, w3)[n % 2][n // 2]).then_inc(w_loaded[n % 4], 16)

            sp.wait_ge(conn_dve, 3)
            sp.wait_ge(consts_set, 1)
            sp.dma_start(w2_sb[:], w2.rearrange("e (j p) d -> p e j d", p=P)).then_inc(ffn_loaded, 16)
            sp.wait_ge(zero_ready, 1)
            sp.dma_start(token_rows[T:T + P, :], zero_rows[:]).then_inc(x2_stored, 16)
            sp.dma_start(out[T:T + P, :], zero_rows[:, 0:D]).then_inc(x2_stored, 16)
            for n in range(6):
                load_w(n)
            for c in range(NC):
                for n in range(6 + 2 * c, min(8 + 2 * c, 2 * E)):
                    load_w(n)
                sp.wait_ge(x2_ready, c + 1)
                sp.dma_start(out_rows[:, c * NT:(c + 1) * NT, :], x_tok[:, c * NT:(c + 1) * NT, :]).then_inc(x2_stored, 16)
                sp.wait_ge(x2n_ready, c + 1)
                sp.wait_ge(weights_ready, c + 1)
                sp.dma_start(token_tiles[:, c * NT:(c + 1) * NT, :], x2n[:, c % 2]).then_inc(rows_stored[c % 2], 16)

        @block.gpsimd
        def _(pool):
            nc.gpsimd.memset(neg_half[:], -0.5)
            nc.gpsimd.memset(zero_rows[:], 0.0).then_inc(zero_ready, 1)
            for t in (keysT, valsT):
                nc.gpsimd.memset(t[:, :, 0:PAD], 0.0)
                last = nc.gpsimd.memset(t[:, :, L + PAD:], 0.0)
            last.then_inc(pads_zero, 1)
            pool.wait_ge(pads_zero, 1)
            chain = [0]

            def link(ins):
                chain[0] += 1
                ins.then_inc(pool_done, 1)
                pool.wait_ge(pool_done, chain[0])

            def normalise(c, which, mv, src, dst, ready):
                r, m = rstd[:, which], nmean[:, which]
                if c:
                    pool.wait_ge(ready, c)
                link(nc.gpsimd.tensor_scalar(r, mv[:, :, 1], EPS, None, ALU.add))
                nc.gpsimd.tensor_scalar(m, mv[:, :, 0], -1.0, None, ALU.mult)
                link(nc.gpsimd.tensor_tensor(r, r, neg_half[:], ALU.pow))
                for t in range(NT):
                    last = nc.gpsimd.tensor_scalar(dst[:, t, :], src[:, t, :], m[:, t:t + 1], r[:, t:t + 1],
                                                   ALU.add, ALU.mult)
                last.then_inc(ready, 1)

            def weigh(c):
                if c == 0:
                    pool.wait_ge(conn_ready, 1)
                pool.wait_ge(exp_ready, c + 1)
                if c >= 1:
                    pool.wait_ge(fw_ready, c)
                nc.gpsimd.tensor_tensor(weighted, expd, conn[:].rearrange("p (a n) -> p a n", a=1).to_broadcast([P, NT, WH]),
                                        ALU.mult).then_inc(weighted_ready, 1)

            def ln1(c):
                pool.wait_ge(ln1_stats, c + 1)
                if c >= 2:
                    pool.wait_ge(x_turned, c - 1)
                normalise(c, 0, mean_var1[:, c % 2], x_tok[:, c * NT:(c + 1) * NT, :], xn[:, c % 2], xn_ready)

            def add_bias(c):
                if c == 0:
                    pool.wait_ge(small_loaded, SMALL)
                pool.wait_ge(xn_ready, c + 1)
                nc.gpsimd.tensor_tensor(x_tok[:, c * NT:(c + 1) * NT, :], x_tok[:, c * NT:(c + 1) * NT, :],
                                        bo_sb[:].rearrange("p (a n) -> p a n", a=1).to_broadcast([P, NT, D]), ALU.add).then_inc(bias_added, 1)

            def ln2(c):
                pool.wait_ge(ln2_stats, c + 1)
                if c >= 2:
                    pool.wait_ge(x2_turned, c - 1)
                    pool.wait_ge(rows_stored[c % 2], 16 * (c // 2))
                normalise(c, 1, mean_var2[:, c % 2], x_tok[:, c * NT:(c + 1) * NT, :], x2n[:, c % 2, :, 0:D], x2n_ready)

            def split_w(c, m):
                n = 2 * c + m
                pool.wait_ge(w_hi_ready, n + 1)
                nc.gpsimd.tensor_tensor(w_lo[:, m, c, :], w_raw[:, n % 4, :], w_hi[:, m, c, :].bitcast(F32),
                                        ALU.subtract).then_inc(w_split, 1)

            def add_pair(c, u):
                pool.wait_ge(pv_ready, WIN * c + 2 * u + 2)
                a = 2 * u % 4
                nc.gpsimd.tensor_tensor(pv[:, a, :], pv[:, a, :], pv[:, a + 1, :], ALU.add).then_inc(pair_ready, 1)

            for i in STEPS:
                on(weigh, i + 1)
                on(add_pair, i, 0)
                on(add_bias, i + 1)
                on(split_w, i + 1, 0)
                on(add_pair, i, 1)
                on(ln2, i - 1)
                on(add_pair, i, 2)
                on(ln1, i + 6)
                on(split_w, i + 1, 1)

            pool.wait_ge(table_read, 1)
            for b in range(2):
                pool.wait_ge(rows_stored[b], 16 * (NC // 2))
            pool.wait_ge(x2_stored, 16 * (NC + 2))

            def count(n):
                return n if isinstance(n, int) else pool.to_reg(n)

            def gather(s, i, r):
                pool.wait_ge(xg_turned, s - (RING - 1)) if not isinstance(s, int) or s >= RING else None
                pool.wait_ge(coef_ready, s - (RING - 1)) if not isinstance(s, int) or s >= RING else None
                pool.wait_ge(scattered[r], 16 * i) if not isinstance(s, int) or s >= RING else None
                copied = count(s + 1)
                nc.gpsimd.tensor_copy(meta[r][:], slot_meta[:, bass.ds(s, 1), :].rearrange("p a b -> p (a b)")).then_inc(meta_copied, 1)
                pool.wait_ge(table_read, 1)
                pool.wait_ge(meta_copied, copied)
                nc.gpsimd.indirect_dma_start(out=xg[r], out_offset=None, in_=token_rows[:, :],
                                             in_offset=bass.IndirectOffsetOnAxis(ap=meta[r][:, 0:1].bitcast(U32), axis=0)).then_inc(gathered[r], 16)

            def scatter(s, i, r):
                weighted_rows = count(s + 1)
                earlier = count(16 * (i + 1) if r else 16 * i)
                pool.wait_ge(table_read, 1)
                pool.wait_ge(y_ready, weighted_rows)
                if r:
                    pool.wait_ge(scattered[r - 1], earlier)
                elif not isinstance(i, int) or i:
                    pool.wait_ge(scattered[RING - 1], earlier)
                nc.gpsimd.indirect_dma_start(out=out[:, :], out_offset=bass.IndirectOffsetOnAxis(ap=meta[r][:, 0:1].bitcast(U32), axis=0),
                                             in_=y[r], in_offset=None, compute_op=ALU.add).then_inc(scattered[r], 16)

            tile_steps(pool, -5, SLOTS - 1, [(5, gather), (0, scatter)])
            for r in range(RING):
                pool.wait_ge(scattered[r], 16 * (SLOTS // RING))

        @block.scalar
        def _(act):
            for dst, src in first:
                act.dma_start(dst, src).then_inc(first_loaded, 16)
            for dst, src in conn_first:
                act.dma_start(dst, src).then_inc(conn_loaded, 16)
            for dst, src in small:
                act.dma_start(dst, src).then_inc(small_loaded, 16)

            def connect_1():
                act.wait_ge(conn_dve, 1)
                nc.scalar.activation(c_h1[:], c_h1[:], ACT.Gelu).then_inc(conn_act, 1)

            def connect_2():
                act.wait_ge(conn_dve, 2)
                nc.scalar.activation(c_h2[:], c_h2[:], ACT.Gelu).then_inc(conn_act, 1)

            def connect_3():
                act.wait_ge(conn_dve, 4)
                nc.scalar.activation(c_row[:], c_row[:], ACT.Exp).then_inc(conn_act, 1)

            def xnT_out(c):
                act.wait_ge(x_turned, c + 1)
                if c >= 2:
                    act.wait_ge(projected, 3 * (c - 1))
                nc.scalar.copy(xnT[:, c % 2, :], ps_tr[:]).then_inc(xnT_ready, 1)

            def qkv_out(c):
                b, o = cols(c)
                if c >= 3:
                    act.wait_ge(qk_ready, WIN * (c - 2))
                dst = [queriesT[:, c % 3, :], keysT[:, b, PAD + o:PAD + o + CH], valsT[:, b, PAD + o:PAD + o + CH]]
                for j in range(3):
                    act.wait_ge(projected, 3 * c + j + 1)
                    nc.scalar.copy(dst[j], ps_proj[(3 * c + j) % 2][:]).then_inc(qkv_ready, 1)

            def scoresT_out(c):
                act.wait_ge(scored, WIN * (c + 1))
                if c:
                    act.wait_ge(scores_turned, c)
                nc.scalar.copy(scoresT, ps_score[0:WH, :]).then_inc(scoresT_ready, 1)

            def exp(c):
                act.wait_ge(scores_shifted, c + 1)
                if c >= 1:
                    act.wait_ge(fw_ready, c)
                nc.scalar.activation(expd, shifted, ACT.Exp, scale=float(1.0 / np.sqrt(np.float32(DH)))).then_inc(exp_ready, 1)

            def fwT_out(c):
                act.wait_ge(fw_turned, c + 1)
                if c >= 1:
                    act.wait_ge(spread_done, WIN * c)
                nc.scalar.copy(fwT_hi, ps_fw[0:WH, :]).then_inc(fwT_hi_ready, 1)

            def x2nT_out(c):
                act.wait_ge(x2_turned, c + 1)
                if c:
                    act.wait_ge(logits_done, c)
                nc.scalar.copy(x2nT[:], ps_fw[:]).then_inc(x2nT_ready, 1)

            def gap_out(c):
                act.wait_ge(gap_ready, c + 1)
                if c >= 2:
                    act.wait_ge(weights_ready, c - 1)
                nc.scalar.activation(gap_exp[:, c % 2, :], gap[:, c % 2, :], ACT.Exp).then_inc(gap_exp_ready, 1)

            def w_hi_out(c):
                for n in range(2 * c, 2 * c + 2):
                    act.wait_ge(w_loaded[n % 4], 16 * (n // 4 + 1))
                    nc.scalar.copy(w_hi[:, n % 2, n // 2, :], w_raw[:, n % 4, :]).then_inc(w_hi_ready, 1)

            for i in STEPS:
                on(scoresT_out, i + 1)
                on(xnT_out, i + 5)
                on(qkv_out, i + 4)
                on(exp, i + 1)
                if i == -5:
                    connect_1()
                if i == -4:
                    connect_2()
                if i == -2:
                    connect_3()
                on(x2nT_out, i - 2)
                on(w_hi_out, i + 1)
                on(gap_out, i - 2)
                on(fwT_out, i + 1)

            def silu(s, i, r):
                act.wait_ge(gate_done, s + 1)
                if not isinstance(s, int) or s >= 2:
                    act.wait_ge(hid_ready, s - 1)
                nc.scalar.activation(sil[:, r % 2, :], ps_gate[r % 2][:], ACT.Silu).then_inc(silu_done, 1)

            def hidT_out(s, i, r):
                act.wait_ge(hid_turned, s + 1)
                if not isinstance(s, int) or s >= 2:
                    act.wait_ge(down_done, s - 1)
                nc.scalar.copy(hidT[:, r % 2, :], ps_hid[:]).then_inc(hidT_ready, 1)

            def y_out(s, i, r):
                act.wait_ge(down_done, s + 1)
                act.wait_ge(coef_ready, s + 1)
                if not isinstance(s, int) or s >= RING:
                    act.wait_ge(scattered[r], 16 * i)
                nc.scalar.activation(y[r], ps_y[:, 0:D], ACT.Copy, scale=coef[r][:]).then_inc(y_ready, 1)

            tile_steps(act, -1, SLOTS, [(1, silu), (0, hidT_out), (-1, y_out)])

        @block.vector
        def _(dve):
            chain = [0]

            def link(ins):
                chain[0] += 1
                ins.then_inc(dve_done, 1)
                dve.wait_ge(dve_done, chain[0])

            by_head = "p (w h) -> p h w"

            ends = np.cumsum([CI, CI, CI * CI, CI, CI, 1, 1])
            cw1, cb1, cw2, cb2, cw3, cb3, pos = (conn_p[:, a:b] for a, b in zip([0, *ends], ends))

            def connect_1():
                dve.wait_ge(conn_loaded, CONN)
                nc.vector.scalar_tensor_tensor(out=c_h1[:], in0=cw1, scalar=pos, in1=cb1, op0=ALU.mult, op1=ALU.add).then_inc(conn_dve, 1)

            def connect_2():
                dve.wait_ge(conn_act, 1)
                link(nc.vector.tensor_tensor(c_pre, cw2.rearrange("p (j i) -> p j i", i=CI),
                                             c_h1[:].rearrange("p (a i) -> p a i", a=1).to_broadcast([WH, CI, CI]), ALU.mult))
                link(nc.vector.tensor_reduce(c_h2[:], c_pre, AX.X, ALU.add))
                nc.vector.tensor_tensor(c_h2[:], c_h2[:], cb2, ALU.add).then_inc(conn_dve, 1)

            def connect_3():
                dve.wait_ge(conn_act, 2)
                link(nc.vector.tensor_tensor(c_h2[:], c_h2[:], cw3, ALU.mult))
                link(nc.vector.tensor_reduce(c_out[:], c_h2[:], AX.X, ALU.add))
                link(nc.vector.tensor_tensor(c_out[:], c_out[:], cb3, ALU.add))
                nc.vector.tensor_copy(c_rep[:], c_out[:].to_broadcast([WH, P])).then_inc(conn_dve, 1)

            def consts():
                dve.wait_ge(small_loaded, SMALL)
                nc.vector.tensor_copy(spread[:], spread_raw[:])
                nc.vector.tensor_copy(iota16[:], iota[:, 0:P])
                nc.vector.tensor_copy(count_w16[:], count_w).then_inc(consts_set, 1)

            def connect_4():
                dve.wait_ge(conn_rows, 1)
                link(nc.vector.tensor_reduce(c_max[:], ps_att[:, 0:WH].rearrange(by_head, h=H), AX.X, ALU.max))
                nc.vector.tensor_tensor(c_row[:].rearrange("p (w h) -> p w h", h=H), ps_att[:, 0:WH].rearrange("p (w h) -> p w h", h=H),
                                        c_max[:].rearrange("p (a h) -> p a h", a=1).to_broadcast([P, WIN, H]), ALU.subtract).then_inc(conn_dve, 1)

            def connect_5():
                dve.wait_ge(conn_act, 3)
                link(nc.vector.tensor_reduce(c_sum[:], c_row[:].rearrange(by_head, h=H), AX.X, ALU.add))
                link(nc.vector.reciprocal(c_sum[:], c_sum[:]))
                nc.vector.tensor_tensor(conn[:].rearrange("p (w h) -> p w h", h=H), c_row[:].rearrange("p (w h) -> p w h", h=H),
                                        c_sum[:].rearrange("p (a h) -> p a h", a=1).to_broadcast([P, WIN, H]), ALU.mult).then_inc(conn_ready, 1)

            def moments(src, mv, ready):
                for t in range(NT):
                    last = nc.vector.bn_stats(stats[:, t, :], src[:, t, :])
                link(last)
                for t in range(NT):
                    last = nc.vector.bn_aggr(mv[:, t, :], stats[:, t, :])
                link(last)
                nc.vector.engine_nop().then_inc(ready, 1)

            def ln1(c):
                dve.wait_ge(x_loaded[c], 16)
                if c >= 2:
                    dve.wait_ge(xn_ready, c - 1)
                moments(x_tok[:, c * NT:(c + 1) * NT, :], mean_var1[:, c % 2], ln1_stats)

            def qk(c, w):
                b, o = cols(c)
                if w == 0:
                    dve.wait_ge(pads_zero, 1)
                    dve.wait_ge(qkv_ready, 3 * (c + 2 if c % CPS < CPS - 1 else c + 1))
                n = WIN * c + w
                if n >= 3:
                    dve.wait_ge(scored, n - 2)
                nc.vector.tensor_tensor(prod[:, n % 3, :], queriesT[:, c % 3, :],
                                        keysT[:, b, o + w:o + w + CH], ALU.mult).then_inc(qk_ready, 1)

            s_whn = ps_tr[:, 0:NT * WH]

            def per_head(t):
                return t.rearrange("p t (a h) -> p t a h", a=1).to_broadcast([P, NT, WIN, H])

            def softmax_a(c):
                dve.wait_ge(scores_turned, c + 1)
                link(nc.vector.tensor_reduce(top_score[:], s_whn.rearrange("p (t w h) -> p t h w", t=NT, w=WIN), AX.X, ALU.max))
                if c >= 1:
                    dve.wait_ge(exp_ready, c)
                nc.vector.tensor_tensor(shifted.rearrange("p t (w h) -> p t w h", h=H),
                                        s_whn.rearrange("p (t w h) -> p t w h", t=NT, w=WIN),
                                        per_head(top_score[:]), ALU.subtract).then_inc(scores_shifted, 1)

            def softmax_b(c):
                dve.wait_ge(exp_ready, c + 1)
                nc.vector.tensor_reduce(sum_exp[:], expd.rearrange("p t (w h) -> p t h w", h=H), AX.X, ALU.add)
                dve.wait_ge(weighted_ready, c + 1)
                link(nc.vector.tensor_reduce(sum_wgt[:], weighted.rearrange("p t (w h) -> p t h w", h=H), AX.X, ALU.add))
                link(nc.vector.scalar_tensor_tensor(out=denom[:], in0=sum_exp[:], scalar=1e-9, in1=sum_wgt[:],
                                                    op0=ALU.mult, op1=ALU.add))
                link(nc.vector.reciprocal(inv_den[:], denom[:]))
                if c >= 1:
                    dve.wait_ge(fw_turned, c)
                nc.vector.tensor_tensor(fw.rearrange("p t (w h) -> p t w h", h=H),
                                        weighted.rearrange("p t (w h) -> p t w h", h=H),
                                        per_head(inv_den[:]), ALU.mult).then_inc(fw_ready, 1)

            def fwT_rest(c):
                dve.wait_ge(fwT_hi_ready, c + 1)
                nc.vector.tensor_tensor(fwT_lo, ps_fw[0:WH, :], fwT_hi.bitcast(F32), ALU.subtract).then_inc(fwT_ready, 1)

            def gate(c):
                ts = slice(c * NT, (c + 1) * NT)
                dve.wait_ge(logits_done, c + 1)
                nc.vector.tensor_tensor(logit[:], ps_fw[:, 0:NT * E].rearrange("p (t e) -> p t e", e=E),
                                        gb_sb[:].rearrange("p (a e) -> p a e", a=1).to_broadcast([P, NT, E]), ALU.add).then_inc(logits_read, 1)
                dve.wait_ge(logits_read, c + 1)
                for t in range(NT):
                    last = nc.vector.max(best[:, t, :], logit[:, t, :])
                link(last)
                for t in range(NT):
                    last = nc.vector.max_index(best_at[:, t, :], best[:, t, :], logit[:, t, :])
                if c >= 2:
                    dve.wait_ge(gap_exp_ready, c - 1)
                nc.vector.tensor_tensor(gap[:, c % 2, :], best[:, :, 1], best[:, :, 0], ALU.subtract).then_inc(gap_ready, 1)
                link(last)
                for k in range(K):
                    last = nc.vector.tensor_tensor(chosen[:, k, :, ts], iota[:, 0:E].rearrange("p (e a) -> p e a", a=1).to_broadcast([P, E, NT]),
                                                   best_at[:, :, k].rearrange("p (a t) -> p a t", a=1).to_broadcast([P, E, NT]), ALU.is_equal)
                link(last)
                nc.vector.tensor_tensor(either[:, :, ts], chosen[:, 0, :, ts], chosen[:, 1, :, ts], ALU.add)

            def weights(c):
                dve.wait_ge(gap_exp_ready, c + 1)
                if c >= 2:
                    dve.wait_ge(rows_stored[c % 2], 16 * (c // 2))
                link(nc.vector.tensor_scalar(one_plus[:], gap_exp[:, c % 2, :], 1.0, None, ALU.add))
                link(nc.vector.reciprocal(x2n[:, c % 2, :, D], one_plus[:]))
                nc.vector.tensor_tensor(x2n[:, c % 2, :, D + 1], gap_exp[:, c % 2, :], x2n[:, c % 2, :, D], ALU.mult).then_inc(weights_ready, 1)

            def pvs(c, w):
                b, o = cols(c)
                n = WIN * c + w
                dve.wait_ge(spread_done, n + 1)
                if w >= 4:
                    dve.wait_ge(wo_done, UNITS * c + (w - 4) // 2 + 1)
                elif c:
                    last_there = max(v for v in range(WIN) if v % 4 == w)
                    dve.wait_ge(wo_done, UNITS * (c - 1) + last_there // 2 + 1)
                nc.vector.tensor_tensor(pv[:, w % 4, :], ps_exp[n % 2][:], valsT[:, b, o + w:o + w + CH],
                                        ALU.mult).then_inc(pv_ready, 1)

            def residual(c):
                dve.wait_ge(wo_done, UNITS * (c + 1))
                dve.wait_ge(bias_added, c + 1)
                xs = x_tok[:, c * NT:(c + 1) * NT, :]
                nc.vector.tensor_tensor(xs, ps_att[:].rearrange("p (t d) -> p t d", t=NT), xs, ALU.add).then_inc(x2_ready, 1)

            def ln2(c):
                xs = x_tok[:, c * NT:(c + 1) * NT, :]
                dve.wait_ge(x2_ready, c + 1)
                if c >= 2:
                    dve.wait_ge(x2n_ready, c - 1)
                moments(xs, mean_var2[:, c % 2], ln2_stats)

            for i in STEPS:
                for w in range(WIN):
                    on(pvs, i, w)
                    on(qk, i + 2 + (w + QLEAD) // WIN, (w + QLEAD) % WIN)
                    if w == 0:
                        on(residual, i - 1)
                    if w == 1:
                        on(softmax_a, i + 1)
                    if w == 2:
                        on(ln2, i - 1)
                    if w == 3:
                        on(softmax_b, i + 1)
                    if w == 4:
                        on(gate, i - 2)
                    if w == 5:
                        on(ln1, i + 6)
                    if w == 6:
                        on(weights, i - 2)
                on(fwT_rest, i + 1)
                if i == -5:
                    connect_1()
                if i == -4:
                    connect_2()
                    consts()
                if i == -3:
                    connect_3()
                if i == -2:
                    connect_4()
                    connect_5()

            dve.wait_ge(counted, 1)
            flat = "p e t -> p (e t)"
            before, count = (ps_count[:, j * E * TILES:(j + 1) * E * TILES].rearrange("p (e t) -> p e t", e=E) for j in range(2))
            link(nc.vector.tensor_tensor_scan(upto.rearrange(flat), reset[:].rearrange(flat), count.rearrange(flat), 0.0, ALU.mult, ALU.add))
            nc.vector.tensor_tensor(ahead, upto, count, ALU.subtract)
            link(nc.vector.tensor_scalar(need_i[:], upto[:, :, TILES - 1], float(P - 1), None, ALU.add))
            link(nc.vector.tensor_scalar(need_i[:], need_i[:], P.bit_length() - 1, None, ALU.arith_shift_right))
            link(nc.vector.tensor_copy(need[:], need_i[:]))
            link(nc.vector.tensor_tensor_scan(need_upto[:], reset[:, 1, 1:1 + E], need[:], 0.0, ALU.mult, ALU.add))
            nc.vector.tensor_tensor(begin[:], need_upto[:], need[:], ALU.subtract)
            link(nc.vector.tensor_tensor(ahead, ahead, before, ALU.add))
            link(nc.vector.scalar_tensor_tensor(out=ahead, in0=begin[:].rearrange("p (e a) -> p e a", a=1).to_broadcast([P, E, TILES]), scalar=float(P),
                                                in1=ahead, op0=ALU.mult, op1=ALU.add))
            for k in range(K):
                last = nc.vector.tensor_tensor(place_of[:, k], chosen[:, k], ahead, ALU.mult)
            link(last)
            link(nc.vector.tensor_reduce(slot[:], place_of[:].rearrange("p k e t -> p k t e"), AX.X, ALU.add))
            link(nc.vector.tensor_copy(slot_i[:, 0], slot[:]))
            nc.vector.tensor_scalar(slot_i[:, 1], slot_i[:, 0], P.bit_length() - 1, None, ALU.arith_shift_right)
            link(nc.vector.tensor_scalar(slot_i[:, 2], slot_i[:, 0], P - 1, None, ALU.bitwise_and))
            nc.vector.tensor_copy(slot_tile[:], slot_i[:, 1])
            link(nc.vector.tensor_copy(slot_part[:], slot_i[:, 2]))
            G = 8
            for g in range(0, K * TILES, G):
                for n in range(g, g + G):
                    k, t = divmod(n, TILES)
                    nc.vector.tensor_scalar(part_hot[:, n, :], iota16[:], slot_part[:, k, t:t + 1], None, ALU.is_equal)
                    last = nc.vector.tensor_scalar(tile_hot[:, n, 0, :], iota16[:, 0:SLOTS], slot_tile[:, k, t:t + 1], float(n + 1),
                                                   ALU.is_equal, ALU.mult)
                link(last)
                nc.vector.tensor_scalar(tile_hot[:, g:g + G, 1, :], tile_hot[:, g:g + G, 0, :], 1.0, own, ALU.min, ALU.mult).then_inc(hots_ready, 1)
            link(nc.vector.tensor_tensor(passed, need_upto[0:1].rearrange("p (a e) -> p a e", a=1).to_broadcast([1, SLOTS, E]),
                                         iota[0:1, 0:SLOTS].rearrange("p (s a) -> p s a", a=1).to_broadcast([1, SLOTS, E]), ALU.is_le))
            link(nc.vector.tensor_reduce(expert_f[:], passed, AX.X, ALU.add))
            link(nc.vector.tensor_scalar(expert_of[:], expert_f[:], float(E - 1), None, ALU.min))
            dve.wait_ge(table_done, 1)
            tab_tile, tab_part = ps_count[:, 0:SLOTS], ps_count[:, SLOTS:2 * SLOTS]
            link(nc.vector.tensor_scalar(empty, tab_tile, 0.0, None, ALU.is_equal))
            nc.vector.scalar_tensor_tensor(out=from_tile, in0=empty, scalar=float(K * TILES + 1), in1=tab_tile, op0=ALU.mult, op1=ALU.add)
            link(nc.vector.scalar_tensor_tensor(out=from_part, in0=empty, scalar=own, in1=tab_part, op0=ALU.mult, op1=ALU.add))
            link(nc.vector.tensor_scalar(second, from_tile, float(TILES + 1), None, ALU.is_ge))
            link(nc.vector.scalar_tensor_tensor(out=token, in0=second, scalar=-float(TILES), in1=from_tile, op0=ALU.mult, op1=ALU.add))
            link(nc.vector.tensor_scalar(token, token, -1.0, float(P), ALU.add, ALU.mult))
            nc.vector.tensor_scalar(slot_meta[:, :, 1].bitcast(F32), second, -2.0, 2.0, ALU.mult, ALU.add)
            link(nc.vector.tensor_tensor(slot_meta[:, :, 0], token, from_part, ALU.add))
            nc.vector.engine_nop().then_inc(table_read, 1)

            def split_x(s, i, r):
                dve.wait_ge(xg_turned, s + 1)
                if not isinstance(s, int) or s >= 2:
                    dve.wait_ge(up_done, s - 1)
                link_x(nc.vector.tensor_copy(x_hi[:, r % 2, :], ps_x[:, 0:P]), s)
                nc.vector.tensor_tensor(x_lo[:, r % 2, :], ps_x[:, 0:P], x_hi[:, r % 2, :].bitcast(F32), ALU.subtract).then_inc(xg_split, 1)

            def link_x(ins, s):
                ins.then_inc(x_hi_ready, 1)
                dve.wait_ge(x_hi_ready, s + 1)

            def weigh(s, i, r):
                dve.wait_ge(gathered[r], 16 * (i + 1))
                if not isinstance(s, int) or s >= RING:
                    dve.wait_ge(y_ready, s - (RING - 1))
                nc.vector.scalar_tensor_tensor(out=coef[r][:], in0=xg[r][:, D + 1:D + 2], scalar=meta[r][:, 1:2].bitcast(F32),
                                               in1=xg[r][:, D:D + 1], op0=ALU.add, op1=ALU.min).then_inc(coef_ready, 1)

            def hidden(s, i, r):
                dve.wait_ge(silu_done, s + 1)
                dve.wait_ge(up_done, s + 1)
                if not isinstance(s, int) or s >= 2:
                    dve.wait_ge(hid_turned, s - 1)
                nc.vector.tensor_tensor(hid[:, r % 2, :], sil[:, r % 2, :], ps_up[r % 2][:], ALU.mult).then_inc(hid_ready, 1)

            tile_steps(dve, -2, SLOTS - 1, [(2, split_x), (2, weigh), (1, hidden)])

        @block.tensor
        def _(pe):
            pe.wait_ge(first_loaded, FIRST)

            def connect():
                pe.wait_ge(conn_dve, 3)
                nc.tensor.matmul(ps_att[:, 0:WH], c_rep[:], ident[0:WH, 0:WH], start=True, stop=True).then_inc(conn_rows, 1)

            def turn(c):
                pe.wait_ge(xn_ready, c + 1)
                if c:
                    pe.wait_ge(xnT_ready, c)
                if c >= 5:
                    pe.wait_ge(scores_shifted, c - 4)
                for t in range(NT):
                    last = nc.tensor.transpose(ps_tr[:, t * P:(t + 1) * P], xn[:, c % 2, t, :], ident[:])
                last.then_inc(x_turned, 1)

            def project(c):
                pe.wait_ge(xnT_ready, c + 1)
                for j, w in enumerate((wq_sb, wk_sb, wv_sb)):
                    n = 3 * c + j
                    if n >= 2:
                        pe.wait_ge(qkv_ready, n - 1)
                    nc.tensor.matmul(ps_proj[n % 2][:], w[:], xnT[:, c % 2, :], start=True, stop=True).then_inc(projected, 1)

            def score(c, w):
                n = WIN * c + w
                if w == 0 and c:
                    pe.wait_ge(scoresT_ready, c)
                pe.wait_ge(qk_ready, n + 1)
                at = (WIN - 1 - w) * H
                nc.tensor.matmul(ps_score[0:WH, :], heads[:, at:at + WH], prod[:, n % 3, :], start=(w == 0), stop=(w == WIN - 1)).then_inc(scored, 1)

            def turn_scores(c):
                pe.wait_ge(scoresT_ready, c + 1)
                pe.wait_ge(xnT_ready, min(c + 5, NC))
                for t in range(NT):
                    last = nc.tensor.transpose(ps_tr[:, t * WH:(t + 1) * WH], scoresT[:, t * P:(t + 1) * P], ident[0:WH, 0:WH])
                last.then_inc(scores_turned, 1)

            def turn2(c):
                pe.wait_ge(x2n_ready, c + 1)
                pe.wait_ge(fwT_ready, min(c + 3, NC))
                if c:
                    pe.wait_ge(logits_read, c)
                for t in range(NT):
                    last = nc.tensor.transpose(ps_fw[:, t * P:(t + 1) * P], x2n[:, c % 2, t, 0:D], ident[:])
                last.then_inc(x2_turned, 1)

            def turn_fw(c):
                pe.wait_ge(fw_ready, c + 1)
                if c >= 3:
                    pe.wait_ge(logits_read, c - 2)
                for t in range(NT):
                    last = nc.tensor.transpose(ps_fw[0:WH, t * P:(t + 1) * P], fw[:, t, :], ident[:])
                last.then_inc(fw_turned, 1)

            def choose(c):
                pe.wait_ge(x2nT_ready, c + 1)
                for t in range(NT):
                    last = nc.tensor.matmul(ps_fw[:, t * E:(t + 1) * E], x2nT[:, t * P:(t + 1) * P], gw_sb[:], start=True, stop=True)
                last.then_inc(logits_done, 1)

            def spread_w(c, w):
                if w == 0:
                    pe.wait_ge(fwT_ready, c + 1)
                n = WIN * c + w
                if n >= 2:
                    pe.wait_ge(pv_ready, n - 1)
                nc.tensor.matmul(ps_exp[n % 2][:], spread[:, w, :], fwT_hi, start=True, stop=False)
                nc.tensor.matmul(ps_exp[n % 2][:], spread[:, w, :], fwT_lo, start=False, stop=True).then_inc(spread_done, 1)

            def out_unit(c, u):
                w = 2 * u
                if w + 1 < WIN:
                    pe.wait_ge(pair_ready, (UNITS - 1) * c + u + 1)
                else:
                    pe.wait_ge(pv_ready, WIN * (c + 1))
                if u == 0 and c:
                    pe.wait_ge(x2_ready, c)
                for t in range(NT):
                    last = nc.tensor.matmul(ps_att[:, t * D:(t + 1) * D], pv[:, w % 4, t * P:(t + 1) * P], wo_sb[:],
                                            start=(w == 0 and t == 0), stop=(w == WIN - 1 and t == NT - 1),
                                            skip_group_check=True)
                last.then_inc(wo_done, 1)

            for i in STEPS:
                on(spread_w, i, 0)
                on(spread_w, i, 1)
                on(turn, i + 5)
                on(project, i + 4)
                if i == -2:
                    connect()
                on(turn_scores, i + 1)
                for w in range(WIN):
                    on(score, i + 2, w)
                    if w == 0:
                        on(turn2, i - 2)
                    if w == 1:
                        on(choose, i - 2)
                    if w >= 3 and w % 2 == 1:
                        on(out_unit, i, w // 2 - 1)
                    if w == 5:
                        on(turn_fw, i + 1)
                    if w + 2 < WIN:
                        on(spread_w, i, w + 2)
                on(out_unit, i, UNITS - 2)
                on(out_unit, i, UNITS - 1)

            pe.wait_ge(weights_ready, NC)
            for j in range(2):
                last = nc.tensor.matmul(ps_count[:, j * E * TILES:(j + 1) * E * TILES], count_w16[:, j, :],
                                        either[:].rearrange("p e t -> p (e t)"), start=True, stop=True)
            last.then_inc(counted, 1)
            G = 8
            for g in range(K * TILES // G):
                pe.wait_ge(hots_ready, g + 1)
                for n in range(g * G, g * G + G):
                    last = nc.tensor.matmul(ps_count[:, 0:2 * SLOTS], part_hot[:, n, :], tile_hot[:, n].rearrange("p a s -> p (a s)"),
                                            start=(n == 0), stop=(n == K * TILES - 1))
            last.then_inc(table_done, 1)
            pe.wait_ge(ffn_loaded, 16)
            pe.wait_ge(w_split, 2 * E)
            pe.wait_ge(table_read, 1)

            def turn_x(s, i, r):
                pe.wait_ge(gathered[r], 16 * (i + 1))
                if not isinstance(s, int) or s >= 1:
                    pe.wait_ge(xg_split, s)
                nc.tensor.transpose(ps_x[:, 0:P], xg[r][:, 0:D], ident[:]).then_inc(xg_turned, 1)

            def expert(s):
                return nc.tensor.value_load(expert_of[0:1, bass.ds(s, 1)], min_val=0, max_val=E - 1)

            def up(s, i, r):
                e = expert(s)
                pe.wait_ge(xg_split, s + 1)
                if not isinstance(s, int) or s >= 2:
                    pe.wait_ge(hid_ready, s - 1)
                for m, (dst, done) in enumerate(((ps_gate, gate_done), (ps_up, up_done))):
                    hi, lo = (w[:, m, bass.ds(e, 1), :].rearrange("p a f -> p (a f)") for w in (w_hi, w_lo))
                    nc.tensor.matmul(dst[r % 2][:], x_hi[:, r % 2, :], hi, start=True, stop=False)
                    nc.tensor.matmul(dst[r % 2][:], x_hi[:, r % 2, :], lo, start=False, stop=False)
                    nc.tensor.matmul(dst[r % 2][:], x_lo[:, r % 2, :], hi, start=False, stop=True).then_inc(done, 1)

            def turn_hid(s, i, r):
                pe.wait_ge(hid_ready, s + 1)
                if not isinstance(s, int) or s >= 1:
                    pe.wait_ge(hidT_ready, s)
                for j in range(FC):
                    last = nc.tensor.transpose(ps_hid[:, j * P:(j + 1) * P], hid[:, r % 2, j * P:(j + 1) * P], ident[:])
                last.then_inc(hid_turned, 1)

            def down(s, i, r):
                e = expert(s)
                pe.wait_ge(hidT_ready, s + 1)
                if not isinstance(s, int) or s >= 1:
                    pe.wait_ge(y_ready, s)
                for j in range(FC):
                    last = nc.tensor.matmul(ps_y[:, 0:D], hidT[:, r % 2, j * P:(j + 1) * P],
                                            w2_sb[:, bass.ds(e, 1), j, :].rearrange("p a d -> p (a d)"), start=(j == 0), stop=(j == FC - 1))
                last.then_inc(down_done, 1)

            tile_steps(pe, -2, SLOTS, [(2, turn_x), (1, up), (0, turn_hid), (-1, down)])


def kernel(**inputs):
    import concourse.bacc as bacc
    from concourse.bass_utils import run_bass_kernel_spmd

    g = {k: np.asarray(v) for k, v in inputs.items()}
    a = {k[8:]: v for k, v in g.items() if k.startswith("L0_attn_")}
    f = {k[7:]: v for k, v in g.items() if k.startswith("L0_ffn_")}

    def rows(v):
        return np.ascontiguousarray(np.broadcast_to(v.reshape(1, -1), (P, v.size)))

    def per_place(v):
        v = v.reshape(H, -1)
        return np.broadcast_to(v[None], (WIN,) + v.shape).reshape(WH, -1)

    pos = np.repeat(np.linspace(0.0, 1.0, WIN, dtype=np.float32), H)[:, None]
    ident = np.eye(P, dtype=np.float32)
    heads = np.repeat(np.eye(H, dtype=np.float32), DH, axis=0)
    wide_heads = np.zeros((P, (2 * WIN - 1) * H), np.float32)
    wide_heads[:, (WIN - 1) * H:WIN * H] = heads
    spread = np.zeros((WIN, H, WIN, P), np.float32)
    for w in range(WIN):
        spread[w, :, w, :] = heads.T
    tokens = a["x"].shape[0] * a["x"].shape[1]
    reset = np.ones((P, f["w1"].shape[0], tokens // P), np.float32)
    reset[:, :, 0] = 0.0
    arrays = {
        "x": a["x"], "wqT": a["wq"].T, "wkT": a["wk"].T, "wvT": a["wv"].T, "woT": a["wo"].T, "bo": rows(a["bo"]),
        "conn": np.concatenate([per_place(a[k]) for k in ("cw1", "cb1", "cw2", "cb2", "cw3", "cb3")] + [pos], axis=1),
        "gate_w": f["gate_w"], "gate_b": rows(f["gate_b"]), "w1": f["w1"], "w3": f["w3"], "w2": f["w2"],
        "ident": ident, "heads": wide_heads, "spread": spread.reshape(WH, WIN, P),
        "iota": np.concatenate([np.broadcast_to(np.arange(P, dtype=np.float32), (P, P)), np.arange(P, dtype=np.float32)[:, None]], axis=1),
        "count": np.stack([np.triu(np.ones((P, P), np.float32), 1), np.ones((P, P), np.float32)], axis=1),
        "reset": reset,
    }
    arrays = {k: np.ascontiguousarray(v) for k, v in arrays.items()}
    nc = bacc.Bacc("TRN2", target_bir_lowering=False, num_devices=1)
    args = [nc.dram_tensor(f"in_{k}", v.shape, mybir.dt.from_np(v.dtype), kind="ExternalInput").ap() for k, v in arrays.items()]
    out = nc.dram_tensor("out_y", (tokens + P, P), F32, kind="ExternalOutput").ap()
    build(nc, *args, out)
    r = run_bass_kernel_spmd(nc, [{f"in_{k}": v for k, v in arrays.items()}], core_ids=[0])
    return r.results[0]["out_y"][:tokens].reshape(a["x"].shape)
```

```python
import numpy as np
from contextlib import ExitStack

import concourse.bass as bass
from concourse import mybir

P = 128
F32 = mybir.dt.float32
F32R = mybir.dt.float32r
BF16 = mybir.dt.bfloat16
I32 = mybir.dt.int32
U32 = mybir.dt.uint32
ALU = mybir.AluOpType
ACT = mybir.ActivationFunctionType
AX = mybir.AxisListType

H = 16
DH = P // H
WIN = 7
PAD = WIN // 2
WH = WIN * H
EPS = 1e-5
RING = 8
UNROLL = 16


def build(nc, x, wqT, wkT, wvT, woT, bo, conn_in, gate_w, gate_b, w1, w3, w2, ident_in, heads_in, spread_in, iota_in, count_in, reset_in, out):
    B, L, D = x.shape
    T = B * L
    E, _, F = w1.shape
    FC = F // P
    CH = 512
    NT = CH // P
    NC = T // CH
    CPS = L // CH
    TILES = T // P
    CI = 32
    assert D == P and L % CH == 0

    x_rows = x.rearrange("b l d -> (b l) d").rearrange("(n p) d -> p n d", p=P)
    out_rows = out.rearrange("(n p) d -> p n d", p=P)
    K = 2
    SLOTS = K * T // P + E - 1
    G = 8
    GROUPS = K * TILES // G
    PART_BY = [("act", "act", "pool", "dve", "act", "pool", "act", "pool")[g % 8] for g in range(GROUPS)]
    ROW = D + K
    token_rows = nc.dram_tensor("token_rows", (T + P, ROW), F32).ap()
    token_tiles = token_rows.rearrange("(n p) d -> p n d", p=P)

    with ExitStack() as ctx:
        def sb(name, shape, dt=F32):
            return ctx.enter_context(nc.sbuf_tensor(name, shape, dt))

        def bank(name):
            return ctx.enter_context(nc.psum_tensor(name, [P, 512], F32))

        def sem(name):
            return ctx.enter_context(nc.semaphore(name))

        x_tok = sb("x_tok", [P, TILES, D])
        KV = B * (L + 2 * PAD)
        attn_mem = sb("attn_mem", [P, 2 * KV + 3 * CH])
        keysT, valsT = (attn_mem[:, j * KV:(j + 1) * KV].rearrange("p (b l) -> p b l", b=B) for j in range(2))
        queriesT = attn_mem[:, 2 * KV:].rearrange("p (r n) -> p r n", r=3)
        w_hi = sb("w_hi", [P, K, E, F], F32R)
        w_lo = sb("w_lo", [P, K, E, F], F32R)
        w2_sb = sb("w2_sb", [P, E, FC, D])
        wqkv_hi = sb("wqkv_hi", [P, 3, D], F32R)
        wqkv_lo = sb("wqkv_lo", [P, 3, D], F32R)
        wo_sb = sb("wo_sb", [P, D])
        bo_sb = sb("bo_sb", [P, D])
        gw_sb = sb("gw_sb", [P, E])
        gb_sb = sb("gb_sb", [P, E])
        def share(t, shapes):
            flat, at, views = t[:], 0, []
            for parts, *dims in shapes:
                n = int(np.prod(dims))
                names = "abc"[:len(dims)]
                v = flat[0:parts, at:at + n]
                if len(dims) > 1:
                    v = v.rearrange(f"p ({' '.join(names)}) -> p {' '.join(names)}", **dict(zip(names[1:], dims[1:])))
                views.append(v)
                at += n
            return views

        NCI = conn_in.shape[1]
        w_raw_mem = sb("w_raw_mem", [P, 4 * F])
        w_raw, = share(w_raw_mem, [(P, 4, F)])
        conn_p, count_w = share(w_raw_mem, [(WH, NCI), (P, 2, P)])
        products = sb("products", [P, 3 * CH])
        prod, = share(products, [(P, 3, CH)])
        upto, ahead, passed, empty, from_tile, from_part, second, token = share(
            products, [(P, E, TILES), (P, E, TILES), (1, SLOTS, E)] + [(P, SLOTS)] * 5)
        values = sb("values", [P, 4 * CH])
        pv, = share(values, [(P, 4, CH)])
        wqkv, = share(values, [(P, 3, D)])
        y = share(values, [(P, D)] * RING)
        distance = values[:].bitcast(BF16)[:, 0:G * P].rearrange("p (n c) -> p n c", n=G)
        xn_mem = sb("xn_mem", [P, max(2 * NT * D, RING * ROW)])
        xn, = share(xn_mem, [(P, 2, NT, D)])
        xg = share(xn_mem, [(P, ROW)] * RING)
        soft_a, soft_b = (sb(f"soft_{n}", [P, 2 * F]) for n in "ab")
        sil, = share(soft_a, [(P, 2, F)])
        shifted, expd = share(soft_a, [(P, NT, WH)] * 2)
        spread_raw, = share(soft_a, [(WH, WIN, P)])
        hid, = share(soft_b, [(P, 2, F)])
        weighted, fw = share(soft_b, [(P, NT, WH)] * 2)
        place_of_mem, = share(soft_b, [(P, K * E, TILES)])
        place_of = place_of_mem.rearrange("p (k e) t -> p k e t", k=K)
        ident = sb("ident", [P, P])
        heads = sb("heads", [P, (2 * WIN - 1) * H])
        hidT = sb("hidT", [P, 2, F])
        scoresT = hidT[0:WH, 0, :]
        spread = sb("spread", [WH, WIN, P], F32R)
        neg_half = sb("neg_half", [P, NT])

        stats = sb("stats", [P, NT, 6])
        moments1 = sb("moments1", [P, 2, NT, 2])
        moments2 = sb("moments2", [P, 2, NT, 2])
        xnT_hi = sb("xnT_hi", [P, CH], F32R)
        xnT_lo = sb("xnT_lo", [P, CH], F32R)
        top_score = sb("top_score", [P, NT, H])
        sum_exp = sb("sum_exp", [P, NT, H])
        sum_wgt = sb("sum_wgt", [P, NT, H])
        denom = sb("denom", [P, NT, H])
        inv_den = sb("inv_den", [P, NT, H])
        hi_mem = sb("hi_mem", [P, CH], F32R)
        lo_mem = sb("lo_mem", [P, CH], F32R)
        fwT_hi, fwT_lo = (t[0:WH, :] for t in (hi_mem, lo_mem))
        x_hi, x_lo = (t[:, 0:2 * P].rearrange("p (r n) -> p r n", r=2) for t in (hi_mem, lo_mem))
        x2n = sb("x2n", [P, 2, NT, ROW])
        x2nT = sb("x2nT", [P, CH])
        conn = sb("conn", [P, WH])
        c_h1 = sb("c_h1", [WH, CI])
        c_pre = hidT[:].rearrange("p a f -> p (a f)")[0:WH, 0:CI * CI].rearrange("p (j i) -> p j i", j=CI)
        c_h2 = sb("c_h2", [WH, CI])
        c_out = sb("c_out", [WH, 1])
        c_rep = sb("c_rep", [WH, P])
        c_row = sb("c_row", [P, WH])
        c_max = sb("c_max", [P, H])
        c_sum = sb("c_sum", [P, H])
        logit = sb("logit", [P, NT, E])
        best = sb("best", [P, NT, 8])
        best_at = sb("best_at", [P, NT, 8], U32)
        gap = sb("gap", [P, 2, NT])
        gap_exp = sb("gap_exp", [P, 2, NT])
        one_plus = sb("one_plus", [P, NT])
        IOTA = iota_in.shape[1]
        iota = sb("iota", [P, IOTA])
        iota16 = sb("iota16", [P, P], BF16)
        own = iota[:, P:P + 1]
        count_w16 = sb("count_w16", [P, 2, P], BF16)
        reset = sb("reset", [P, E, TILES])
        chosen = sb("chosen", [P, K, E, TILES])
        either = sb("either", [P, E, TILES], BF16)
        need_i = sb("need_i", [P, E], I32)
        need = sb("need", [P, E])
        need_upto = sb("need_upto", [P, E])
        begin = sb("begin", [P, E])
        slot = sb("slot", [P, K, TILES])
        slot_i = sb("slot_i", [P, 3, K, TILES], I32)
        slot_tile = sb("slot_tile", [P, K, TILES])
        slot_part = sb("slot_part", [P, K, TILES])
        hots = attn_mem[:].bitcast(BF16)
        PH = K * TILES * P
        part_hot = hots[:, 0:PH].rearrange("p (n c) -> p n c", c=P)
        tile_hot = hots[:, PH:PH + K * TILES * 2 * SLOTS].rearrange("p (n a s) -> p n a s", a=2, s=SLOTS)
        slot_meta = sb("slot_meta", [P, SLOTS, 2], I32)
        expert_f = sb("expert_f", [1, SLOTS])
        expert_of = sb("expert_of", [1, SLOTS], I32)
        zero_rows = sb("zero_rows", [P, ROW])
        table_pick = sb("table_pick", [P, 1])
        meta = [sb(f"meta{r}", [P, 2], I32) for r in range(RING)]
        coef = [sb(f"coef{r}", [P, 1]) for r in range(RING)]

        ps_tr = bank("ps_tr")
        ps_fw = bank("ps_fw")
        ps_proj = [bank(f"ps_proj{i}") for i in range(2)]
        ps_score = bank("ps_score")
        ps_exp = [bank(f"ps_exp{i}") for i in range(2)]
        ps_att = bank("ps_att")

        ps_count = ps_score
        ps_x, ps_hid, ps_y = ps_tr, ps_fw, ps_att
        ps_gate, ps_up = ps_proj, ps_exp

        x_loaded = [sem(f"x_loaded{c}") for c in range(NC)]
        first_loaded = sem("first_loaded")
        conn_loaded = sem("conn_loaded")
        small_loaded = sem("small_loaded")
        ffn_loaded = sem("ffn_loaded")
        pads_zero = sem("pads_zero")
        consts_set = sem("consts_set")
        dve_done = sem("dve_done")
        rstd_ready = sem("rstd_ready")
        conn_ready = sem("conn_ready")
        conn_act = sem("conn_act")
        conn_dve = sem("conn_dve")
        conn_rows = sem("conn_rows")
        ln1_stats = sem("ln1_stats")
        xn_ready = sem("xn_ready")
        x_turned = sem("x_turned")
        xnT_hi_ready = sem("xnT_hi_ready")
        xnT_ready = sem("xnT_ready")
        wqkv_split = sem("wqkv_split")
        projected = sem("projected")
        qkv_ready = sem("qkv_ready")
        qk_ready = sem("qk_ready")
        qk_by_pool = sem("qk_by_pool")
        ln1_scaled = sem("ln1_scaled")
        ln2_scaled = sem("ln2_scaled")
        scored = sem("scored")
        scoresT_ready = sem("scoresT_ready")
        scores_turned = sem("scores_turned")
        scores_shifted = sem("scores_shifted")
        exp_ready = sem("exp_ready")
        weighted_ready = sem("weighted_ready")
        fw_ready = sem("fw_ready")
        fw_turned = sem("fw_turned")
        fwT_hi_ready = sem("fwT_hi_ready")
        fwT_ready = sem("fwT_ready")
        spread_done = sem("spread_done")
        pv_ready = sem("pv_ready")
        sums_ready = sem("sums_ready")
        wo_done = sem("wo_done")
        bias_added = sem("bias_added")
        x2_ready = sem("x2_ready")
        ln2_stats = sem("ln2_stats")
        x2n_ready = sem("x2n_ready")
        x2_turned = sem("x2_turned")
        x2nT_ready = sem("x2nT_ready")
        logits_done = sem("logits_done")
        logits_read = sem("logits_read")
        gap_ready = sem("gap_ready")
        gap_exp_ready = sem("gap_exp_ready")
        weights_ready = sem("weights_ready")
        w_loaded = [sem(f"w_loaded{i}") for i in range(4)]
        w_hi_ready = sem("w_hi_ready")
        w_split = sem("w_split")
        zero_ready = sem("zero_ready")
        rows_stored = [sem(f"rows_stored{i}") for i in range(2)]
        x2_stored = sem("x2_stored")
        counted = sem("counted")
        hots_ready = sem("hots_ready")
        places_ready = sem("places_ready")
        part_by_pool = sem("part_by_pool")
        part_by_act = sem("part_by_act")
        distance_ready = sem("distance_ready")
        experts_ready = sem("experts_ready")
        table_done = sem("table_done")
        table_read = sem("table_read")
        meta_copied = sem("meta_copied")
        gathered = [sem(f"gathered{r}") for r in range(RING)]
        scattered = [sem(f"scattered{r}") for r in range(RING)]
        coef_ready = sem("coef_ready")
        xg_turned = sem("xg_turned")
        x_hi_ready = sem("x_hi_ready")
        xg_split = sem("xg_split")
        gate_done = sem("gate_done")
        up_done = sem("up_done")
        silu_done = sem("silu_done")
        hid_ready = sem("hid_ready")
        hid_turned = sem("hid_turned")
        hidT_ready = sem("hidT_ready")
        down_done = sem("down_done")
        y_ready = sem("y_ready")

        first = [(ident[:], ident_in), *((wqkv[:, j, :], w) for j, w in enumerate((wqT, wkT, wvT)))]
        conn_first = [(conn_p, conn_in), (heads[:], heads_in)]
        small = [(bo_sb[:], bo), (spread_raw, spread_in), (wo_sb[:], woT), (gw_sb[:], gate_w),
                 (gb_sb[:], gate_b), (iota[:], iota_in), (count_w, count_in), (reset[:], reset_in)]
        FIRST = 16 * len(first)
        CONN = 16 * len(conn_first)
        SMALL = 16 * len(small)
        STEPS = range(-6, NC + 2)

        def tile_steps(eng, first, last, stages):
            leads = [lead for lead, _ in stages]
            lo = max(-(-max(first, -min(leads)) // UNROLL), 1)
            hi = (SLOTS - max(max(leads), 0)) // UNROLL

            def step(i, u, ends):
                for lead, stage in stages:
                    if not ends or 0 <= UNROLL * i + u + lead < SLOTS:
                        turns, r = divmod(u + lead, RING)
                        stage(UNROLL * i + (u + lead), UNROLL // RING * i + turns, r)

            for s in range(first, UNROLL * lo):
                step(s // UNROLL, s % UNROLL, True)
            with eng.Fori(lo, hi) as i:
                for u in range(UNROLL):
                    step(i, u, False)
            for s in range(UNROLL * hi, last + 1):
                step(s // UNROLL, s % UNROLL, True)

        block = ctx.enter_context(nc.Block())

        POOL_W = (1, 2, 5)
        QLEAD = 1

        def on(stage, c, *w):
            if 0 <= c < NC:
                stage(c, *w)

        ADDS = [(1, 0, 2), (3, 2, 4), (3, 1, 4), (1, 0, 6)]
        QUAD, LAST = 2, 3
        UNITS = [(3, QUAD), (1, LAST), (2, None)]

        def cols(c):
            return c // CPS, (c % CPS) * CH

        @block.sync
        def _(sp):
            for c in range(NC):
                if c == 3:
                    for dst, src in small:
                        sp.dma_start(dst, src).then_inc(small_loaded, 16)
                sp.dma_start(x_tok[:, c * NT:(c + 1) * NT, :], x_rows[:, c * NT:(c + 1) * NT, :]).then_inc(x_loaded[c], 16)

            def load_w(n):
                if n >= 4:
                    sp.wait_ge(w_split, n - 3)
                sp.dma_start(w_raw[:, n % 4, :], (w1, w3)[n % 2][n // 2]).then_inc(w_loaded[n % 4], 16)

            sp.wait_ge(conn_dve, 3)
            sp.wait_ge(consts_set, 1)
            sp.dma_start(w2_sb[:], w2.rearrange("e (j p) d -> p e j d", p=P)).then_inc(ffn_loaded, 16)
            sp.wait_ge(zero_ready, 1)
            sp.dma_start(token_rows[T:T + P, :], zero_rows[:]).then_inc(x2_stored, 16)
            sp.dma_start(out[T:T + P, :], zero_rows[:, 0:D]).then_inc(x2_stored, 16)
            for n in range(6):
                load_w(n)
            for c in range(NC):
                for n in range(6 + 2 * c, min(8 + 2 * c, 2 * E)):
                    load_w(n)
                sp.wait_ge(x2_ready, c + 1)
                sp.dma_start(out_rows[:, c * NT:(c + 1) * NT, :], x_tok[:, c * NT:(c + 1) * NT, :]).then_inc(x2_stored, 16)
                sp.wait_ge(x2n_ready, c + 1)
                sp.wait_ge(weights_ready, c + 1)
                sp.dma_start(token_tiles[:, c * NT:(c + 1) * NT, :], x2n[:, c % 2]).then_inc(rows_stored[c % 2], 16)

        @block.gpsimd
        def _(pool):
            nc.gpsimd.memset(neg_half[:], -0.5)
            nc.gpsimd.memset(zero_rows[:], 0.0).then_inc(zero_ready, 1)
            for t in (keysT, valsT):
                nc.gpsimd.memset(t[:, :, 0:PAD], 0.0)
                last = nc.gpsimd.memset(t[:, :, L + PAD:], 0.0)
            last.then_inc(pads_zero, 1)
            pool.wait_ge(pads_zero, 1)
            norms = [0]

            def scale_and_bias(mv, ready):
                nc.gpsimd.tensor_tensor(mv[:, :, 1], mv[:, :, 1], neg_half[:], ALU.pow).then_inc(rstd_ready, 1)
                norms[0] += 1
                pool.wait_ge(rstd_ready, norms[0])
                nc.gpsimd.tensor_tensor(mv[:, :, 0], mv[:, :, 0], mv[:, :, 1], ALU.mult).then_inc(ready, 1)

            def weigh(c):
                if c == 0:
                    pool.wait_ge(conn_ready, 1)
                pool.wait_ge(exp_ready, c + 1)
                if c >= 1:
                    pool.wait_ge(fw_ready, c)
                nc.gpsimd.tensor_tensor(weighted, expd, conn[:].rearrange("p (a n) -> p a n", a=1).to_broadcast([P, NT, WH]),
                                        ALU.mult).then_inc(weighted_ready, 1)

            def ln1(c):
                pool.wait_ge(ln1_stats, c + 1)
                scale_and_bias(moments1[:, c % 2], ln1_scaled)

            def add_bias(c):
                if c == 0:
                    pool.wait_ge(small_loaded, SMALL)
                pool.wait_ge(xn_ready, c + 1)
                nc.gpsimd.tensor_tensor(x_tok[:, c * NT:(c + 1) * NT, :], x_tok[:, c * NT:(c + 1) * NT, :],
                                        bo_sb[:].rearrange("p (a n) -> p a n", a=1).to_broadcast([P, NT, D]), ALU.add).then_inc(bias_added, 1)

            def ln2(c):
                pool.wait_ge(ln2_stats, c + 1)
                scale_and_bias(moments2[:, c % 2], ln2_scaled)

            def qk(c, w):
                if w == POOL_W[0]:
                    pool.wait_ge(qkv_ready, 3 * (c + 2 if c % CPS < CPS - 1 else c + 1))
                b, o = cols(c)
                n = WIN * c + w
                if n >= 3:
                    pool.wait_ge(scored, n - 2)
                nc.gpsimd.tensor_tensor(prod[:, n % 3, :], queriesT[:, c % 3, :],
                                        keysT[:, b, o + w:o + w + CH], ALU.mult).then_inc(qk_by_pool, 1)

            def split_w(c, m):
                n = 2 * c + m
                pool.wait_ge(w_hi_ready, n + 1)
                nc.gpsimd.tensor_tensor(w_lo[:, m, c, :], w_raw[:, n % 4, :], w_hi[:, m, c, :].bitcast(F32),
                                        ALU.subtract).then_inc(w_split, 1)

            def add(c, n):
                at, src, products_needed = ADDS[n]
                pool.wait_ge(pv_ready, WIN * c + products_needed)
                if n == QUAD:
                    pool.wait_ge(sums_ready, len(ADDS) * c + n)
                nc.gpsimd.tensor_tensor(pv[:, at, :], pv[:, at, :], pv[:, src, :], ALU.add).then_inc(sums_ready, 1)

            for i in STEPS:
                on(qk, i + 2, 1)
                on(qk, i + 2, 2)
                on(ln2, i - 1)
                on(add, i, 0)
                on(weigh, i + 1)
                on(qk, i + 2, 5)
                on(add, i, 1)
                on(add, i, QUAD)
                on(add, i, 3)
                on(ln1, i + 6)
                on(add_bias, i + 1)
                on(split_w, i + 1, 0)
                on(split_w, i + 1, 1)

            pool.wait_ge(places_ready, 1)
            for g in range(GROUPS):
                if PART_BY[g] == "pool":
                    for n in range(g * G, (g + 1) * G):
                        k, t = divmod(n, TILES)
                        last = nc.gpsimd.tensor_scalar(part_hot[:, n, :], iota16[:], slot_part[:, k, t:t + 1], None, ALU.is_equal)
                    last.then_inc(part_by_pool, 1)

            pool.wait_ge(table_read, 1)
            for b in range(2):
                pool.wait_ge(rows_stored[b], 16 * (NC // 2))
            pool.wait_ge(x2_stored, 16 * (NC + 2))

            def count(n):
                return n if isinstance(n, int) else pool.to_reg(n)

            def gather(s, i, r):
                pool.wait_ge(xg_turned, s - (RING - 1)) if not isinstance(s, int) or s >= RING else None
                pool.wait_ge(coef_ready, s - (RING - 1)) if not isinstance(s, int) or s >= RING else None
                pool.wait_ge(scattered[r], 16 * i) if not isinstance(s, int) or s >= RING else None
                copied = count(s + 1)
                nc.gpsimd.tensor_copy(meta[r][:], slot_meta[:, bass.ds(s, 1), :].rearrange("p a b -> p (a b)")).then_inc(meta_copied, 1)
                pool.wait_ge(table_read, 1)
                pool.wait_ge(meta_copied, copied)
                nc.gpsimd.indirect_dma_start(out=xg[r], out_offset=None, in_=token_rows[:, :],
                                             in_offset=bass.IndirectOffsetOnAxis(ap=meta[r][:, 0:1].bitcast(U32), axis=0)).then_inc(gathered[r], 16)

            def scatter(s, i, r):
                weighted_rows = count(s + 1)
                earlier = count(16 * (i + 1) if r else 16 * i)
                pool.wait_ge(table_read, 1)
                pool.wait_ge(y_ready, weighted_rows)
                if r:
                    pool.wait_ge(scattered[r - 1], earlier)
                elif not isinstance(i, int) or i:
                    pool.wait_ge(scattered[RING - 1], earlier)
                nc.gpsimd.indirect_dma_start(out=out[:, :], out_offset=bass.IndirectOffsetOnAxis(ap=meta[r][:, 0:1].bitcast(U32), axis=0),
                                             in_=y[r], in_offset=None, compute_op=ALU.add).then_inc(scattered[r], 16)

            tile_steps(pool, -5, SLOTS - 1, [(5, gather), (0, scatter)])
            for r in range(RING):
                pool.wait_ge(scattered[r], 16 * len(range(r, SLOTS, RING)))

        @block.scalar
        def _(act):
            act.wait_ge(zero_ready, 1)
            nc.scalar.activation(table_pick[:], zero_rows[:, 0:1], ACT.Gelu)
            for dst, src in first:
                act.dma_start(dst, src).then_inc(first_loaded, 16)
            for dst, src in conn_first:
                act.dma_start(dst, src).then_inc(conn_loaded, 16)

            def connect_1():
                act.wait_ge(conn_dve, 1)
                nc.scalar.activation(c_h1[:], c_h1[:], ACT.Gelu).then_inc(conn_act, 1)

            def connect_2():
                act.wait_ge(conn_dve, 2)
                nc.scalar.activation(c_h2[:], c_h2[:], ACT.Gelu).then_inc(conn_act, 1)

            def connect_3():
                act.wait_ge(conn_dve, 4)
                nc.scalar.activation(c_row[:], c_row[:], ACT.Exp).then_inc(conn_act, 1)

            def normalise(mv, src, dst, ready):
                for t in range(NT):
                    last = nc.scalar.activation(dst[:, t, :], src[:, t, :], ACT.Identity, scale=mv[:, t, 1:2], bias=mv[:, t, 0:1])
                last.then_inc(ready, 1)

            def ln1(c):
                act.wait_ge(ln1_scaled, c + 1)
                if c >= 2:
                    act.wait_ge(x_turned, c - 1)
                normalise(moments1[:, c % 2], x_tok[:, c * NT:(c + 1) * NT, :], xn[:, c % 2], xn_ready)

            def ln2(c):
                act.wait_ge(ln2_scaled, c + 1)
                if c >= 2:
                    act.wait_ge(x2_turned, c - 1)
                    act.wait_ge(rows_stored[c % 2], 16 * (c // 2))
                normalise(moments2[:, c % 2], x_tok[:, c * NT:(c + 1) * NT, :], x2n[:, c % 2, :, 0:D], x2n_ready)

            def xnT_out(c):
                act.wait_ge(x_turned, c + 1)
                if c:
                    act.wait_ge(projected, 3 * c)
                nc.scalar.copy(xnT_hi[:], ps_tr[:]).then_inc(xnT_hi_ready, 1)

            def qkv_out(c):
                b, o = cols(c)
                if c >= 3:
                    act.wait_ge(scored, WIN * (c - 2))
                dst = [queriesT[:, c % 3, :], keysT[:, b, PAD + o:PAD + o + CH], valsT[:, b, PAD + o:PAD + o + CH]]
                for j in range(3):
                    act.wait_ge(projected, 3 * c + j + 1)
                    nc.scalar.copy(dst[j], ps_proj[(3 * c + j) % 2][:]).then_inc(qkv_ready, 1)

            def scoresT_out(c):
                act.wait_ge(scored, WIN * (c + 1))
                if c:
                    act.wait_ge(scores_turned, c)
                nc.scalar.copy(scoresT, ps_score[0:WH, :]).then_inc(scoresT_ready, 1)

            def exp(c):
                act.wait_ge(scores_shifted, c + 1)
                if c >= 1:
                    act.wait_ge(fw_ready, c)
                nc.scalar.activation(expd, shifted, ACT.Exp, scale=float(1.0 / np.sqrt(np.float32(DH)))).then_inc(exp_ready, 1)

            def fwT_out(c):
                act.wait_ge(fw_turned, c + 1)
                if c >= 1:
                    act.wait_ge(spread_done, WIN * c)
                nc.scalar.copy(fwT_hi, ps_fw[0:WH, :]).then_inc(fwT_hi_ready, 1)

            def x2nT_out(c):
                act.wait_ge(x2_turned, c + 1)
                if c:
                    act.wait_ge(logits_done, c)
                nc.scalar.copy(x2nT[:], ps_fw[:]).then_inc(x2nT_ready, 1)

            def gap_out(c):
                act.wait_ge(gap_ready, c + 1)
                if c >= 2:
                    act.wait_ge(weights_ready, c - 1)
                nc.scalar.activation(gap_exp[:, c % 2, :], gap[:, c % 2, :], ACT.Exp).then_inc(gap_exp_ready, 1)

            def w_hi_out(c):
                for n in range(2 * c, 2 * c + 2):
                    act.wait_ge(w_loaded[n % 4], 16 * (n // 4 + 1))
                    nc.scalar.copy(w_hi[:, n % 2, n // 2, :], w_raw[:, n % 4, :]).then_inc(w_hi_ready, 1)

            for i in STEPS:
                on(scoresT_out, i + 1)
                on(qkv_out, i + 4)
                on(x2nT_out, i - 2)
                on(exp, i + 1)
                on(w_hi_out, i + 1)
                on(gap_out, i - 2)
                on(xnT_out, i + 5)
                on(fwT_out, i + 1)
                on(ln2, i - 1)
                on(ln1, i + 6)
                if i == -5:
                    connect_1()
                if i == -4:
                    connect_2()
                if i == -2:
                    connect_3()

            act.wait_ge(places_ready, 1)
            done = 0
            for g in range(GROUPS):
                if PART_BY[g] == "act":
                    if done:
                        act.wait_ge(part_by_act, done)
                    for n in range(G):
                        k, t = divmod(g * G + n, TILES)
                        last = nc.scalar.activation(distance[:, n, :], iota16[:], ACT.Abs, scale=-1.0, bias=slot_part[:, k, t:t + 1])
                    last.then_inc(distance_ready, 1)
                    done += 1
                    act.wait_ge(distance_ready, done)
                    nc.scalar.activation(part_hot[:, g * G:(g + 1) * G, :], distance, ACT.Relu, scale=-1.0, bias=1.0).then_inc(part_by_act, 1)

            def silu(s, i, r):
                act.wait_ge(gate_done, s + 1)
                if not isinstance(s, int) or s >= 2:
                    act.wait_ge(hid_ready, s - 1)
                nc.scalar.activation(sil[:, r % 2, :], ps_gate[r % 2][:], ACT.Silu).then_inc(silu_done, 1)

            def hidT_out(s, i, r):
                act.wait_ge(hid_turned, s + 1)
                if not isinstance(s, int) or s >= 2:
                    act.wait_ge(down_done, s - 1)
                nc.scalar.copy(hidT[:, r % 2, :], ps_hid[:]).then_inc(hidT_ready, 1)

            def y_out(s, i, r):
                act.wait_ge(down_done, s + 1)
                act.wait_ge(coef_ready, s + 1)
                if not isinstance(s, int) or s >= RING:
                    act.wait_ge(scattered[r], 16 * i)
                nc.scalar.activation(y[r], ps_y[:, 0:D], ACT.Copy, scale=coef[r][:]).then_inc(y_ready, 1)

            tile_steps(act, -1, SLOTS, [(1, silu), (0, hidT_out), (-1, y_out)])

        @block.vector
        def _(dve):
            chain = [0]

            def link(ins):
                chain[0] += 1
                ins.then_inc(dve_done, 1)
                dve.wait_ge(dve_done, chain[0])

            by_head = "p (w h) -> p h w"

            ends = np.cumsum([CI, CI, CI * CI, CI, CI, 1, 1])
            cw1, cb1, cw2, cb2, cw3, cb3, pos = (conn_p[:, a:b] for a, b in zip([0, *ends], ends))

            def connect_1():
                dve.wait_ge(conn_loaded, CONN)
                nc.vector.scalar_tensor_tensor(out=c_h1[:], in0=cw1, scalar=pos, in1=cb1, op0=ALU.mult, op1=ALU.add).then_inc(conn_dve, 1)

            def connect_2():
                dve.wait_ge(conn_act, 1)
                link(nc.vector.tensor_tensor(c_pre, cw2.rearrange("p (j i) -> p j i", i=CI),
                                             c_h1[:].rearrange("p (a i) -> p a i", a=1).to_broadcast([WH, CI, CI]), ALU.mult))
                link(nc.vector.tensor_reduce(c_h2[:], c_pre, AX.X, ALU.add))
                nc.vector.tensor_tensor(c_h2[:], c_h2[:], cb2, ALU.add).then_inc(conn_dve, 1)

            def connect_3():
                dve.wait_ge(conn_act, 2)
                link(nc.vector.tensor_tensor(c_h2[:], c_h2[:], cw3, ALU.mult))
                link(nc.vector.tensor_reduce(c_out[:], c_h2[:], AX.X, ALU.add))
                link(nc.vector.tensor_tensor(c_out[:], c_out[:], cb3, ALU.add))
                nc.vector.tensor_copy(c_rep[:], c_out[:].to_broadcast([WH, P])).then_inc(conn_dve, 1)

            def consts():
                dve.wait_ge(small_loaded, SMALL)
                nc.vector.tensor_copy(spread[:], spread_raw[:])
                nc.vector.tensor_copy(iota16[:], iota[:, 0:P])
                nc.vector.tensor_copy(count_w16[:], count_w).then_inc(consts_set, 1)

            def connect_4():
                dve.wait_ge(conn_rows, 1)
                link(nc.vector.tensor_reduce(c_max[:], ps_att[:, 0:WH].rearrange(by_head, h=H), AX.X, ALU.max))
                nc.vector.tensor_tensor(c_row[:].rearrange("p (w h) -> p w h", h=H), ps_att[:, 0:WH].rearrange("p (w h) -> p w h", h=H),
                                        c_max[:].rearrange("p (a h) -> p a h", a=1).to_broadcast([P, WIN, H]), ALU.subtract).then_inc(conn_dve, 1)

            def connect_5():
                dve.wait_ge(conn_act, 3)
                link(nc.vector.tensor_reduce(c_sum[:], c_row[:].rearrange(by_head, h=H), AX.X, ALU.add))
                link(nc.vector.reciprocal(c_sum[:], c_sum[:]))
                nc.vector.tensor_tensor(conn[:].rearrange("p (w h) -> p w h", h=H), c_row[:].rearrange("p (w h) -> p w h", h=H),
                                        c_sum[:].rearrange("p (a h) -> p a h", a=1).to_broadcast([P, WIN, H]), ALU.mult).then_inc(conn_ready, 1)

            def measure(src, mv, ready):
                for t in range(NT):
                    last = nc.vector.bn_stats(stats[:, t, :], src[:, t, :])
                link(last)
                for t in range(NT):
                    last = nc.vector.bn_aggr(mv[:, t, :], stats[:, t, :])
                link(last)
                nc.vector.tensor_scalar(mv[:, :, 0], mv[:, :, 0], -1.0, None, ALU.mult)
                nc.vector.tensor_scalar(mv[:, :, 1], mv[:, :, 1], EPS, None, ALU.add).then_inc(ready, 1)

            def ln1(c):
                dve.wait_ge(x_loaded[c], 16)
                if c >= 2:
                    dve.wait_ge(xn_ready, c - 1)
                measure(x_tok[:, c * NT:(c + 1) * NT, :], moments1[:, c % 2], ln1_stats)

            def split_wqkv():
                dve.wait_ge(first_loaded, FIRST)
                link(nc.vector.tensor_copy(wqkv_hi[:], wqkv))
                nc.vector.tensor_tensor(wqkv_lo[:], wqkv, wqkv_hi[:].bitcast(F32), ALU.subtract).then_inc(wqkv_split, 1)

            def xnT_rest(c):
                dve.wait_ge(xnT_hi_ready, c + 1)
                nc.vector.tensor_tensor(xnT_lo[:], ps_tr[:], xnT_hi[:].bitcast(F32), ALU.subtract).then_inc(xnT_ready, 1)

            def qk(c, w):
                if w in POOL_W:
                    return
                b, o = cols(c)
                if w == 0:
                    dve.wait_ge(pads_zero, 1)
                    dve.wait_ge(qkv_ready, 3 * (c + 2 if c % CPS < CPS - 1 else c + 1))
                n = WIN * c + w
                if n >= 3:
                    dve.wait_ge(scored, n - 2)
                nc.vector.tensor_tensor(prod[:, n % 3, :], queriesT[:, c % 3, :],
                                        keysT[:, b, o + w:o + w + CH], ALU.mult).then_inc(qk_ready, 1)

            s_whn = ps_tr[:, 0:NT * WH]

            def per_head(t):
                return t.rearrange("p t (a h) -> p t a h", a=1).to_broadcast([P, NT, WIN, H])

            def softmax_a(c):
                dve.wait_ge(scores_turned, c + 1)
                link(nc.vector.tensor_reduce(top_score[:], s_whn.rearrange("p (t w h) -> p t h w", t=NT, w=WIN), AX.X, ALU.max))
                if c >= 1:
                    dve.wait_ge(exp_ready, c)
                nc.vector.tensor_tensor(shifted.rearrange("p t (w h) -> p t w h", h=H),
                                        s_whn.rearrange("p (t w h) -> p t w h", t=NT, w=WIN),
                                        per_head(top_score[:]), ALU.subtract).then_inc(scores_shifted, 1)

            def softmax_b(c):
                dve.wait_ge(exp_ready, c + 1)
                link(nc.vector.tensor_reduce(sum_exp[:], expd.rearrange("p t (w h) -> p t h w", h=H), AX.X, ALU.add))

            def softmax_c(c):
                dve.wait_ge(weighted_ready, c + 1)
                link(nc.vector.tensor_reduce(sum_wgt[:], weighted.rearrange("p t (w h) -> p t h w", h=H), AX.X, ALU.add))
                link(nc.vector.scalar_tensor_tensor(out=denom[:], in0=sum_exp[:], scalar=1e-9, in1=sum_wgt[:],
                                                    op0=ALU.mult, op1=ALU.add))
                link(nc.vector.reciprocal(inv_den[:], denom[:]))
                if c >= 1:
                    dve.wait_ge(fw_turned, c)
                nc.vector.tensor_tensor(fw.rearrange("p t (w h) -> p t w h", h=H),
                                        weighted.rearrange("p t (w h) -> p t w h", h=H),
                                        per_head(inv_den[:]), ALU.mult).then_inc(fw_ready, 1)

            def fwT_rest(c):
                dve.wait_ge(fwT_hi_ready, c + 1)
                nc.vector.tensor_tensor(fwT_lo, ps_fw[0:WH, :], fwT_hi.bitcast(F32), ALU.subtract).then_inc(fwT_ready, 1)

            def gate(c):
                ts = slice(c * NT, (c + 1) * NT)
                dve.wait_ge(logits_done, c + 1)
                nc.vector.tensor_tensor(logit[:], ps_fw[:, 0:NT * E].rearrange("p (t e) -> p t e", e=E),
                                        gb_sb[:].rearrange("p (a e) -> p a e", a=1).to_broadcast([P, NT, E]), ALU.add).then_inc(logits_read, 1)
                dve.wait_ge(logits_read, c + 1)
                for t in range(NT):
                    last = nc.vector.max(best[:, t, :], logit[:, t, :])
                link(last)
                for t in range(NT):
                    last = nc.vector.max_index(best_at[:, t, :], best[:, t, :], logit[:, t, :])
                if c >= 2:
                    dve.wait_ge(gap_exp_ready, c - 1)
                nc.vector.tensor_tensor(gap[:, c % 2, :], best[:, :, 1], best[:, :, 0], ALU.subtract).then_inc(gap_ready, 1)
                link(last)

            def choices(c):
                ts = slice(c * NT, (c + 1) * NT)
                for k in range(K):
                    last = nc.vector.tensor_tensor(chosen[:, k, :, ts], iota[:, 0:E].rearrange("p (e a) -> p e a", a=1).to_broadcast([P, E, NT]),
                                                   best_at[:, :, k].rearrange("p (a t) -> p a t", a=1).to_broadcast([P, E, NT]), ALU.is_equal)
                link(last)
                nc.vector.tensor_tensor(either[:, :, ts], chosen[:, 0, :, ts], chosen[:, 1, :, ts], ALU.add)

            def weights(c):
                dve.wait_ge(gap_exp_ready, c + 1)
                if c >= 2:
                    dve.wait_ge(rows_stored[c % 2], 16 * (c // 2))
                link(nc.vector.tensor_scalar(one_plus[:], gap_exp[:, c % 2, :], 1.0, None, ALU.add))
                link(nc.vector.reciprocal(x2n[:, c % 2, :, D], one_plus[:]))
                nc.vector.tensor_tensor(x2n[:, c % 2, :, D + 1], gap_exp[:, c % 2, :], x2n[:, c % 2, :, D], ALU.mult).then_inc(weights_ready, 1)

            def pvs(c, w):
                b, o = cols(c)
                n = WIN * c + w
                dve.wait_ge(spread_done, n + 1)
                if w >= 4:
                    dve.wait_ge(sums_ready, len(ADDS) * c + {4: 0, 5: QUAD, 6: 1}[w] + 1)
                elif c and w == 0:
                    dve.wait_ge(sums_ready, len(ADDS) * c)
                elif c:
                    dve.wait_ge(wo_done, len(UNITS) * (c - 1) + {1: 2, 2: 3, 3: 1}[w])
                nc.vector.tensor_tensor(pv[:, w % 4, :], ps_exp[n % 2][:], valsT[:, b, o + w:o + w + CH],
                                        ALU.mult).then_inc(pv_ready, 1)

            def residual(c):
                dve.wait_ge(wo_done, len(UNITS) * (c + 1))
                dve.wait_ge(bias_added, c + 1)
                xs = x_tok[:, c * NT:(c + 1) * NT, :]
                nc.vector.tensor_tensor(xs, ps_att[:].rearrange("p (t d) -> p t d", t=NT), xs, ALU.add).then_inc(x2_ready, 1)

            def ln2(c):
                xs = x_tok[:, c * NT:(c + 1) * NT, :]
                dve.wait_ge(x2_ready, c + 1)
                if c >= 2:
                    dve.wait_ge(x2n_ready, c - 1)
                measure(xs, moments2[:, c % 2], ln2_stats)

            for i in STEPS:
                for w in range(WIN):
                    on(pvs, i, w)
                    on(qk, i + 2 + (w + QLEAD) // WIN, (w + QLEAD) % WIN)
                    if w == 0:
                        on(residual, i - 1)
                        on(ln2, i - 1)
                    if w == 1:
                        on(ln1, i + 6)
                        on(softmax_a, i + 1)
                    if w == 2:
                        on(softmax_b, i + 1)
                    if w == 4:
                        on(softmax_c, i + 1)
                        on(gate, i - 2)
                    if w == 5:
                        on(xnT_rest, i + 5)
                        on(choices, i - 2)
                    if w == 6:
                        on(weights, i - 2)
                on(fwT_rest, i + 1)
                if i == STEPS[0]:
                    split_wqkv()
                if i == -5:
                    connect_1()
                if i == -4:
                    connect_2()
                if i == -3:
                    connect_3()
                    consts()
                if i == -2:
                    connect_4()
                    connect_5()

            dve.wait_ge(counted, 1)
            flat = "p e t -> p (e t)"
            before, count = (ps_count[:, j * E * TILES:(j + 1) * E * TILES].rearrange("p (e t) -> p e t", e=E) for j in range(2))
            link(nc.vector.tensor_tensor_scan(upto.rearrange(flat), reset[:].rearrange(flat), count.rearrange(flat), 0.0, ALU.mult, ALU.add))
            nc.vector.tensor_tensor(ahead, upto, count, ALU.subtract)
            link(nc.vector.tensor_scalar(need_i[:], upto[:, :, TILES - 1], float(P - 1), None, ALU.add))
            link(nc.vector.tensor_scalar(need_i[:], need_i[:], P.bit_length() - 1, None, ALU.arith_shift_right))
            link(nc.vector.tensor_copy(need[:], need_i[:]))
            link(nc.vector.tensor_tensor_scan(need_upto[:], reset[:, 1, 1:1 + E], need[:], 0.0, ALU.mult, ALU.add))
            nc.vector.tensor_tensor(begin[:], need_upto[:], need[:], ALU.subtract)
            link(nc.vector.tensor_tensor(ahead, ahead, before, ALU.add))
            link(nc.vector.scalar_tensor_tensor(out=ahead, in0=begin[:].rearrange("p (e a) -> p e a", a=1).to_broadcast([P, E, TILES]), scalar=float(P),
                                                in1=ahead, op0=ALU.mult, op1=ALU.add))
            for k in range(K):
                last = nc.vector.tensor_tensor(place_of[:, k], chosen[:, k], ahead, ALU.mult)
            link(last)
            link(nc.vector.tensor_reduce(slot[:], place_of[:].rearrange("p k e t -> p k t e"), AX.X, ALU.add))
            link(nc.vector.tensor_copy(slot_i[:, 0], slot[:]))
            nc.vector.tensor_scalar(slot_i[:, 1], slot_i[:, 0], P.bit_length() - 1, None, ALU.arith_shift_right)
            link(nc.vector.tensor_scalar(slot_i[:, 2], slot_i[:, 0], P - 1, None, ALU.bitwise_and))
            nc.vector.tensor_copy(slot_tile[:], slot_i[:, 1])
            link(nc.vector.tensor_copy(slot_part[:], slot_i[:, 2]))
            nc.vector.engine_nop().then_inc(places_ready, 1)
            for g in range(GROUPS):
                for n in range(g * G, (g + 1) * G):
                    k, t = divmod(n, TILES)
                    if PART_BY[g] == "dve":
                        nc.vector.tensor_scalar(part_hot[:, n, :], iota16[:], slot_part[:, k, t:t + 1], None, ALU.is_equal)
                    last = nc.vector.tensor_scalar(tile_hot[:, n, 0, :], iota16[:, 0:SLOTS], slot_tile[:, k, t:t + 1], float(n + 1),
                                                   ALU.is_equal, ALU.mult)
                link(last)
                ns = slice(g * G, (g + 1) * G)
                nc.vector.tensor_scalar(tile_hot[:, ns, 1, :], tile_hot[:, ns, 0, :], 1.0, own, ALU.min, ALU.mult).then_inc(hots_ready, 1)
            dve.wait_ge(table_done, 1)
            tab_tile, tab_part = ps_count[:, 0:SLOTS], ps_count[:, SLOTS:2 * SLOTS]
            link(nc.vector.tensor_scalar(empty, tab_tile, 0.0, None, ALU.is_equal))
            nc.vector.scalar_tensor_tensor(out=from_tile, in0=empty, scalar=float(K * TILES + 1), in1=tab_tile, op0=ALU.mult, op1=ALU.add)
            link(nc.vector.scalar_tensor_tensor(out=from_part, in0=empty, scalar=own, in1=tab_part, op0=ALU.mult, op1=ALU.add))
            link(nc.vector.tensor_scalar(second, from_tile, float(TILES + 1), None, ALU.is_ge))
            link(nc.vector.scalar_tensor_tensor(out=token, in0=second, scalar=-float(TILES), in1=from_tile, op0=ALU.mult, op1=ALU.add))
            link(nc.vector.tensor_scalar(token, token, -1.0, float(P), ALU.add, ALU.mult))
            nc.vector.tensor_scalar(slot_meta[:, :, 1].bitcast(F32), second, -2.0, 2.0, ALU.mult, ALU.add)
            link(nc.vector.tensor_tensor(slot_meta[:, :, 0], token, from_part, ALU.add))
            nc.vector.engine_nop().then_inc(table_read, 1)
            link(nc.vector.tensor_tensor(passed, need_upto[0:1].rearrange("p (a e) -> p a e", a=1).to_broadcast([1, SLOTS, E]),
                                         iota[0:1, 0:SLOTS].rearrange("p (s a) -> p s a", a=1).to_broadcast([1, SLOTS, E]), ALU.is_le))
            link(nc.vector.tensor_reduce(expert_f[:], passed, AX.X, ALU.add))
            nc.vector.tensor_scalar(expert_of[:], expert_f[:], float(E - 1), None, ALU.min).then_inc(experts_ready, 1)

            def split_x(s, i, r):
                dve.wait_ge(xg_turned, s + 1)
                if not isinstance(s, int) or s >= 2:
                    dve.wait_ge(up_done, s - 1)
                link_x(nc.vector.tensor_copy(x_hi[:, r % 2, :], ps_x[:, 0:P]), s)
                nc.vector.tensor_tensor(x_lo[:, r % 2, :], ps_x[:, 0:P], x_hi[:, r % 2, :].bitcast(F32), ALU.subtract).then_inc(xg_split, 1)

            def link_x(ins, s):
                ins.then_inc(x_hi_ready, 1)
                dve.wait_ge(x_hi_ready, s + 1)

            def weigh(s, i, r):
                dve.wait_ge(gathered[r], 16 * (i + 1))
                if not isinstance(s, int) or s >= RING:
                    dve.wait_ge(y_ready, s - (RING - 1))
                nc.vector.scalar_tensor_tensor(out=coef[r][:], in0=xg[r][:, D + 1:D + 2], scalar=meta[r][:, 1:2].bitcast(F32),
                                               in1=xg[r][:, D:D + 1], op0=ALU.add, op1=ALU.min).then_inc(coef_ready, 1)

            def hidden(s, i, r):
                dve.wait_ge(silu_done, s + 1)
                dve.wait_ge(up_done, s + 1)
                if not isinstance(s, int) or s >= 2:
                    dve.wait_ge(hid_turned, s - 1)
                nc.vector.tensor_tensor(hid[:, r % 2, :], sil[:, r % 2, :], ps_up[r % 2][:], ALU.mult).then_inc(hid_ready, 1)

            tile_steps(dve, -2, SLOTS - 1, [(2, split_x), (2, weigh), (1, hidden)])

        @block.tensor
        def _(pe):
            pe.wait_ge(first_loaded, FIRST)

            def connect():
                pe.wait_ge(conn_dve, 3)
                nc.tensor.matmul(ps_att[:, 0:WH], c_rep[:], ident[0:WH, 0:WH], start=True, stop=True).then_inc(conn_rows, 1)

            def turn(c):
                pe.wait_ge(xn_ready, c + 1)
                if c:
                    pe.wait_ge(xnT_ready, c)
                if c >= 4:
                    pe.wait_ge(scores_shifted, c - 3)
                for t in range(NT):
                    last = nc.tensor.transpose(ps_tr[:, t * P:(t + 1) * P], xn[:, c % 2, t, :], ident[:])
                last.then_inc(x_turned, 1)

            def project(c):
                pe.wait_ge(xnT_ready, c + 1)
                if c == 0:
                    pe.wait_ge(wqkv_split, 1)
                for j in range(3):
                    n = 3 * c + j
                    if n >= 2:
                        pe.wait_ge(qkv_ready, n - 1)
                    nc.tensor.matmul(ps_proj[n % 2][:], wqkv_hi[:, j, :], xnT_hi[:], start=True, stop=False)
                    nc.tensor.matmul(ps_proj[n % 2][:], wqkv_hi[:, j, :], xnT_lo[:], start=False, stop=False)
                    nc.tensor.matmul(ps_proj[n % 2][:], wqkv_lo[:, j, :], xnT_hi[:], start=False, stop=True).then_inc(projected, 1)

            def score(c, w):
                n = WIN * c + w
                if w == 0 and c:
                    pe.wait_ge(scoresT_ready, c)
                if w in POOL_W:
                    pe.wait_ge(qk_by_pool, len(POOL_W) * c + POOL_W.index(w) + 1)
                else:
                    pe.wait_ge(qk_ready, (WIN - len(POOL_W)) * c + w + 1 - sum(v < w for v in POOL_W))
                at = (WIN - 1 - w) * H
                nc.tensor.matmul(ps_score[0:WH, :], heads[:, at:at + WH], prod[:, n % 3, :], start=(w == 0), stop=(w == WIN - 1)).then_inc(scored, 1)

            def turn_scores(c):
                pe.wait_ge(scoresT_ready, c + 1)
                pe.wait_ge(xnT_ready, min(c + 4, NC))
                for t in range(NT):
                    last = nc.tensor.transpose(ps_tr[:, t * WH:(t + 1) * WH], scoresT[:, t * P:(t + 1) * P], ident[0:WH, 0:WH])
                last.then_inc(scores_turned, 1)

            def turn2(c):
                pe.wait_ge(x2n_ready, c + 1)
                pe.wait_ge(fwT_ready, min(c + 3, NC))
                if c:
                    pe.wait_ge(logits_read, c)
                for t in range(NT):
                    last = nc.tensor.transpose(ps_fw[:, t * P:(t + 1) * P], x2n[:, c % 2, t, 0:D], ident[:])
                last.then_inc(x2_turned, 1)

            def turn_fw(c):
                pe.wait_ge(fw_ready, c + 1)
                if c >= 3:
                    pe.wait_ge(logits_read, c - 2)
                for t in range(NT):
                    last = nc.tensor.transpose(ps_fw[0:WH, t * P:(t + 1) * P], fw[:, t, :], ident[:])
                last.then_inc(fw_turned, 1)

            def choose(c):
                pe.wait_ge(x2nT_ready, c + 1)
                for t in range(NT):
                    last = nc.tensor.matmul(ps_fw[:, t * E:(t + 1) * E], x2nT[:, t * P:(t + 1) * P], gw_sb[:], start=True, stop=True)
                last.then_inc(logits_done, 1)

            def spread_w(c, w):
                if w == 0:
                    pe.wait_ge(fwT_ready, c + 1)
                n = WIN * c + w
                if n >= 2:
                    pe.wait_ge(pv_ready, n - 1)
                nc.tensor.matmul(ps_exp[n % 2][:], spread[:, w, :], fwT_hi, start=True, stop=False)
                nc.tensor.matmul(ps_exp[n % 2][:], spread[:, w, :], fwT_lo, start=False, stop=True).then_inc(spread_done, 1)

            def out_unit(c, u):
                at, add = UNITS[u]
                if add is None:
                    pe.wait_ge(pv_ready, WIN * (c + 1))
                else:
                    pe.wait_ge(sums_ready, len(ADDS) * c + add + 1)
                if u == 0 and c:
                    pe.wait_ge(x2_ready, c)
                for t in range(NT):
                    last = nc.tensor.matmul(ps_att[:, t * D:(t + 1) * D], pv[:, at, t * P:(t + 1) * P], wo_sb[:],
                                            start=(u == 0 and t == 0), stop=(u == len(UNITS) - 1 and t == NT - 1),
                                            skip_group_check=True)
                last.then_inc(wo_done, 1)

            for i in STEPS:
                on(spread_w, i, 0)
                on(spread_w, i, 1)
                on(project, i + 4)
                if i == -2:
                    connect()
                on(turn_scores, i + 1)
                on(turn2, i - 2)
                for w in range(WIN):
                    on(score, i + 2, w)
                    if w == 2:
                        on(choose, i - 2)
                    if w == 3:
                        on(turn, i + 5)
                    if w == 5:
                        on(out_unit, i, 0)
                        on(turn_fw, i + 1)
                    if w + 2 < WIN:
                        on(spread_w, i, w + 2)
                on(out_unit, i, 2)
                on(out_unit, i, 1)

            pe.wait_ge(weights_ready, NC)
            for j in range(2):
                last = nc.tensor.matmul(ps_count[:, j * E * TILES:(j + 1) * E * TILES], count_w16[:, j, :],
                                        either[:].rearrange("p e t -> p (e t)"), start=True, stop=True)
            last.then_inc(counted, 1)
            for g in range(GROUPS):
                pe.wait_ge(hots_ready, g + 1)
                if PART_BY[g] == "pool":
                    pe.wait_ge(part_by_pool, PART_BY[:g + 1].count("pool"))
                if PART_BY[g] == "act":
                    pe.wait_ge(part_by_act, PART_BY[:g + 1].count("act"))
                for n in range(g * G, g * G + G):
                    last = nc.tensor.matmul(ps_count[:, 0:2 * SLOTS], part_hot[:, n, :], tile_hot[:, n].rearrange("p a s -> p (a s)"),
                                            start=(n == 0), stop=(n == K * TILES - 1))
            last.then_inc(table_done, 1)
            pe.wait_ge(ffn_loaded, 16)
            pe.wait_ge(w_split, 2 * E)
            pe.wait_ge(table_read, 1)
            pe.wait_ge(experts_ready, 1)

            def turn_x(s, i, r):
                pe.wait_ge(gathered[r], 16 * (i + 1))
                if not isinstance(s, int) or s >= 1:
                    pe.wait_ge(xg_split, s)
                nc.tensor.transpose(ps_x[:, 0:P], xg[r][:, 0:D], ident[:]).then_inc(xg_turned, 1)

            def expert(s):
                return nc.tensor.value_load(expert_of[0:1, bass.ds(s, 1)], min_val=0, max_val=E - 1)

            def up(s, i, r):
                e = expert(s)
                pe.wait_ge(xg_split, s + 1)
                if not isinstance(s, int) or s >= 2:
                    pe.wait_ge(hid_ready, s - 1)
                for m, (dst, done) in enumerate(((ps_gate, gate_done), (ps_up, up_done))):
                    hi, lo = (w[:, m, bass.ds(e, 1), :].rearrange("p a f -> p (a f)") for w in (w_hi, w_lo))
                    nc.tensor.matmul(dst[r % 2][:], x_hi[:, r % 2, :], hi, start=True, stop=False)
                    nc.tensor.matmul(dst[r % 2][:], x_hi[:, r % 2, :], lo, start=False, stop=False)
                    nc.tensor.matmul(dst[r % 2][:], x_lo[:, r % 2, :], hi, start=False, stop=True).then_inc(done, 1)

            def turn_hid(s, i, r):
                pe.wait_ge(hid_ready, s + 1)
                if not isinstance(s, int) or s >= 1:
                    pe.wait_ge(hidT_ready, s)
                for j in range(FC):
                    last = nc.tensor.transpose(ps_hid[:, j * P:(j + 1) * P], hid[:, r % 2, j * P:(j + 1) * P], ident[:])
                last.then_inc(hid_turned, 1)

            def down(s, i, r):
                e = expert(s)
                pe.wait_ge(hidT_ready, s + 1)
                if not isinstance(s, int) or s >= 1:
                    pe.wait_ge(y_ready, s)
                for j in range(FC):
                    last = nc.tensor.matmul(ps_y[:, 0:D], hidT[:, r % 2, j * P:(j + 1) * P],
                                            w2_sb[:, bass.ds(e, 1), j, :].rearrange("p a d -> p (a d)"), start=(j == 0), stop=(j == FC - 1))
                last.then_inc(down_done, 1)

            tile_steps(pe, -2, SLOTS, [(2, turn_x), (1, up), (0, turn_hid), (-1, down)])


def kernel(**inputs):
    import concourse.bacc as bacc
    from concourse.bass_utils import run_bass_kernel_spmd

    g = {k: np.asarray(v) for k, v in inputs.items()}
    a = {k[8:]: v for k, v in g.items() if k.startswith("L0_attn_")}
    f = {k[7:]: v for k, v in g.items() if k.startswith("L0_ffn_")}

    def rows(v):
        return np.ascontiguousarray(np.broadcast_to(v.reshape(1, -1), (P, v.size)))

    def per_place(v):
        v = v.reshape(H, -1)
        return np.broadcast_to(v[None], (WIN,) + v.shape).reshape(WH, -1)

    pos = np.repeat(np.linspace(0.0, 1.0, WIN, dtype=np.float32), H)[:, None]
    ident = np.eye(P, dtype=np.float32)
    heads = np.repeat(np.eye(H, dtype=np.float32), DH, axis=0)
    wide_heads = np.zeros((P, (2 * WIN - 1) * H), np.float32)
    wide_heads[:, (WIN - 1) * H:WIN * H] = heads
    spread = np.zeros((WIN, H, WIN, P), np.float32)
    for w in range(WIN):
        spread[w, :, w, :] = heads.T
    tokens = a["x"].shape[0] * a["x"].shape[1]
    reset = np.ones((P, f["w1"].shape[0], tokens // P), np.float32)
    reset[:, :, 0] = 0.0
    arrays = {
        "x": a["x"], "wqT": a["wq"].T, "wkT": a["wk"].T, "wvT": a["wv"].T, "woT": a["wo"].T, "bo": rows(a["bo"]),
        "conn": np.concatenate([per_place(a[k]) for k in ("cw1", "cb1", "cw2", "cb2", "cw3", "cb3")] + [pos], axis=1),
        "gate_w": f["gate_w"], "gate_b": rows(f["gate_b"]), "w1": f["w1"], "w3": f["w3"], "w2": f["w2"],
        "ident": ident, "heads": wide_heads, "spread": spread.reshape(WH, WIN, P),
        "iota": np.concatenate([np.broadcast_to(np.arange(P, dtype=np.float32), (P, P)), np.arange(P, dtype=np.float32)[:, None]], axis=1),
        "count": np.stack([np.triu(np.ones((P, P), np.float32), 1), np.ones((P, P), np.float32)], axis=1),
        "reset": reset,
    }
    arrays = {k: np.ascontiguousarray(v) for k, v in arrays.items()}
    nc = bacc.Bacc("TRN2", target_bir_lowering=False, num_devices=1)
    args = [nc.dram_tensor(f"in_{k}", v.shape, mybir.dt.from_np(v.dtype), kind="ExternalInput").ap() for k, v in arrays.items()]
    out = nc.dram_tensor("out_y", (tokens + P, P), F32, kind="ExternalOutput").ap()
    build(nc, *args, out)
    r = run_bass_kernel_spmd(nc, [{f"in_{k}": v for k, v in arrays.items()}], core_ids=[0])
    return r.results[0]["out_y"][:tokens].reshape(a["x"].shape)
```
